# Optimizing a Trainium2 kernel written in Bass

```python
import numpy as np
import jax
import jax.numpy as jnp

def _softmax(x, axis=-1):
    return jax.nn.softmax(x, axis=axis)

def _gelu(x):
    return jax.nn.gelu(x, approximate=True)

def _silu(x):
    return jax.nn.silu(x)

def _sigmoid(x):
    return jax.nn.sigmoid(x)

def _layernorm(x, axis=-1, eps=1e-05):
    m = jnp.mean(x, axis=axis, keepdims=True)
    v = jnp.var(x, axis=axis, keepdims=True)
    return (x - m) / jnp.sqrt(v + eps)

def _scatter_add(tgt, idx, src, axis=0):
    return tgt.at[idx].add(src)

def _segment_sum(src, seg, n):
    return jax.ops.segment_sum(src, seg, n)
kernel_name = 'mk_cond_resid_d4_seqx_r2_4183fe'

def setup_inputs(seed: int=0):
    np.random.seed(seed)
    _w = jnp.asarray

    def _rec_inputs():
        import jax
        import jax.numpy as jnp
        _rk = jax.random.key(seed)
        x = -0.000125 + 0.9999 * jax.random.normal(jax.random.fold_in(_rk, 1), (128, 128, 2048), jnp.float32)
        _lenS = 128 - jax.random.randint(jax.random.fold_in(_rk, 7), (128,), 0, max(1, 128 // 4) + 1, jnp.int32)
        _lenS2 = 128 - jax.random.randint(jax.random.fold_in(_rk, 8), (128,), 0, max(1, 128 // 4) + 1, jnp.int32)
        cond_128 = 0.0061147 + 1.02565 * jax.random.normal(jax.random.fold_in(_rk, 11), (128, 128), jnp.float32)
        fside_S_0 = -0.022604 + 0.987366 * jax.random.normal(jax.random.fold_in(_rk, 12), (128,), jnp.float32)
        return (x, cond_128, fside_S_0)
    x, cond_128, fside_S_0 = _rec_inputs()

    def _L0_cond_setup():
        import jax, jax.numpy as jnp
        import numpy as np
        K = 8
        T = 1.0
        D_EMBD = 128
        IN_C = 128
        OUT_C = 128
        BS = 32
        H = 2048
        HID = 128
        key = jax.random.key(seed)
        ks = jax.random.split(key, 10)
        s = lambda fan_in: 1.0 / np.sqrt(fan_in)
        return {'x': jax.random.normal(ks[0], (BS, IN_C, H), dtype=jnp.float32), 'embedding': jax.random.normal(ks[1], (BS, D_EMBD), dtype=jnp.float32), 'W0': jax.random.normal(ks[2], (D_EMBD, HID), dtype=jnp.float32) * s(D_EMBD), 'b0': jnp.zeros((HID,), dtype=jnp.float32), 'W1': jax.random.normal(ks[3], (HID, HID), dtype=jnp.float32) * s(HID), 'b1': jnp.zeros((HID,), dtype=jnp.float32), 'W2': jax.random.normal(ks[4], (HID, K), dtype=jnp.float32) * s(HID), 'b2': jnp.zeros((K,), dtype=jnp.float32), 'weight': jax.random.normal(ks[5], (K, OUT_C, IN_C, 1), dtype=jnp.float32) * s(IN_C), 'bias_k': jax.random.normal(ks[6], (K, OUT_C), dtype=jnp.float32) * 0.1}
    _L0_cond_all = _L0_cond_setup()
    _L0_cond_in = {k: v for k, v in _L0_cond_all.items() if k in ('W0', 'b0', 'W1', 'b1', 'W2', 'b2', 'weight', 'bias_k')}
    del _L0_cond_all

    def _L1_cond_setup():
        import jax, jax.numpy as jnp
        import numpy as np
        from jax import lax
        N, C_IN, L = (32, 128, 2048)
        C_OUT, K, GROUPS = (128, 9, 4)
        C_DIM, PAD, STRIDE = (128, 4, 1)
        key = jax.random.key(seed)
        k1, k2, k3, k4, k5 = jax.random.split(key, 5)
        x = jax.random.normal(k1, (N, C_IN, L), dtype=jnp.float32)
        c = jax.random.normal(k2, (N, C_DIM), dtype=jnp.float32)
        weight = jax.random.normal(k3, (C_OUT, C_IN // GROUPS, K), dtype=jnp.float32)
        c_weight = jax.random.normal(k4, (C_OUT, C_DIM), dtype=jnp.float32)
        bias = jax.random.normal(k5, (C_OUT,), dtype=jnp.float32)
        return {'x': x, 'c': c, 'weight': weight, 'c_weight': c_weight, 'bias': bias}
    _L1_cond_all = _L1_cond_setup()
    _L1_cond_in = {k: v for k, v in _L1_cond_all.items() if k in ('weight', 'c_weight')}
    del _L1_cond_all

    def _L2_cond_setup():
        import jax, jax.numpy as jnp
        import numpy as np
        K = 8
        T = 1.0
        D_EMBD = 128
        IN_C = 128
        OUT_C = 128
        BS = 32
        H = 2048
        HID = 128
        key = jax.random.key(seed)
        ks = jax.random.split(key, 10)
        s = lambda fan_in: 1.0 / np.sqrt(fan_in)
        return {'x': jax.random.normal(ks[0], (BS, IN_C, H), dtype=jnp.float32), 'embedding': jax.random.normal(ks[1], (BS, D_EMBD), dtype=jnp.float32), 'W0': jax.random.normal(ks[2], (D_EMBD, HID), dtype=jnp.float32) * s(D_EMBD), 'b0': jnp.zeros((HID,), dtype=jnp.float32), 'W1': jax.random.normal(ks[3], (HID, HID), dtype=jnp.float32) * s(HID), 'b1': jnp.zeros((HID,), dtype=jnp.float32), 'W2': jax.random.normal(ks[4], (HID, K), dtype=jnp.float32) * s(HID), 'b2': jnp.zeros((K,), dtype=jnp.float32), 'weight': jax.random.normal(ks[5], (K, OUT_C, IN_C, 1), dtype=jnp.float32) * s(IN_C), 'bias_k': jax.random.normal(ks[6], (K, OUT_C), dtype=jnp.float32) * 0.1}
    _L2_cond_all = _L2_cond_setup()
    _L2_cond_in = {k: v for k, v in _L2_cond_all.items() if k in ('W0', 'b0', 'W1', 'b1', 'W2', 'b2', 'weight', 'bias_k')}
    del _L2_cond_all

    def _L3_cond_setup():
        import jax, jax.numpy as jnp
        import numpy as np
        from jax import lax
        N, C_IN, L = (32, 128, 2048)
        C_OUT, K, GROUPS = (128, 9, 4)
        C_DIM, PAD, STRIDE = (128, 4, 1)
        key = jax.random.key(seed)
        k1, k2, k3, k4, k5 = jax.random.split(key, 5)
        x = jax.random.normal(k1, (N, C_IN, L), dtype=jnp.float32)
        c = jax.random.normal(k2, (N, C_DIM), dtype=jnp.float32)
        weight = jax.random.normal(k3, (C_OUT, C_IN // GROUPS, K), dtype=jnp.float32)
        c_weight = jax.random.normal(k4, (C_OUT, C_DIM), dtype=jnp.float32)
        bias = jax.random.normal(k5, (C_OUT,), dtype=jnp.float32)
        return {'x': x, 'c': c, 'weight': weight, 'c_weight': c_weight, 'bias': bias}
    _L3_cond_all = _L3_cond_setup()
    _L3_cond_in = {k: v for k, v in _L3_cond_all.items() if k in ('weight', 'c_weight')}
    del _L3_cond_all
    return {'x': x, 'cond_128': cond_128, 'fside_S_0': fside_S_0, 'L0_cond_W0': _L0_cond_in['W0'], 'L0_cond_b0': _L0_cond_in['b0'], 'L0_cond_W1': _L0_cond_in['W1'], 'L0_cond_b1': _L0_cond_in['b1'], 'L0_cond_W2': _L0_cond_in['W2'], 'L0_cond_b2': _L0_cond_in['b2'], 'L0_cond_weight': _L0_cond_in['weight'], 'L0_cond_bias_k': _L0_cond_in['bias_k'], 'L1_cond_weight': _L1_cond_in['weight'], 'L1_cond_c_weight': _L1_cond_in['c_weight'], 'L2_cond_W0': _L2_cond_in['W0'], 'L2_cond_b0': _L2_cond_in['b0'], 'L2_cond_W1': _L2_cond_in['W1'], 'L2_cond_b1': _L2_cond_in['b1'], 'L2_cond_W2': _L2_cond_in['W2'], 'L2_cond_b2': _L2_cond_in['b2'], 'L2_cond_weight': _L2_cond_in['weight'], 'L2_cond_bias_k': _L2_cond_in['bias_k'], 'L3_cond_weight': _L3_cond_in['weight'], 'L3_cond_c_weight': _L3_cond_in['c_weight']}

def reference(x, cond_128, fside_S_0, L0_cond_W0, L0_cond_b0, L0_cond_W1, L0_cond_b1, L0_cond_W2, L0_cond_b2, L0_cond_weight, L0_cond_bias_k, L1_cond_weight, L1_cond_c_weight, L2_cond_W0, L2_cond_b0, L2_cond_W1, L2_cond_b1, L2_cond_W2, L2_cond_b2, L2_cond_weight, L2_cond_bias_k, L3_cond_weight, L3_cond_c_weight):
    import jax
    import jax.numpy as jnp

    def _L0_cond_ref(x, embedding, W0, b0, W1, b1, W2, b2, weight, bias_k):
        import jax, jax.numpy as jnp
        import numpy as np
        K = 8
        T = 1.0
        D_EMBD = 128
        IN_C = 128
        OUT_C = 128
        BS = 32
        H = 2048
        HID = 128
        h = jax.nn.gelu(embedding @ W0 + b0, approximate=False)
        h = jax.nn.gelu(h @ W1 + b1, approximate=False)
        att = jax.nn.softmax((h @ W2 + b2) / T, axis=-1)
        agg_w = jnp.einsum('bk,koi->boi', att, weight[..., 0])
        agg_b = att @ bias_k
        out = jnp.einsum('boi,bih->boh', agg_w, x) + agg_b[:, :, None]
        return out

    def _L1_cond_ref(x, c, weight, c_weight, bias):
        import jax, jax.numpy as jnp
        import numpy as np
        from jax import lax
        N, C_IN, L = (32, 128, 2048)
        C_OUT, K, GROUPS = (128, 9, 4)
        C_DIM, PAD, STRIDE = (128, 4, 1)
        out = lax.conv_general_dilated(x, weight, window_strides=(STRIDE,), padding=[(PAD, PAD)], dimension_numbers=('NCH', 'OIH', 'NCH'), feature_group_count=GROUPS)
        ctx = jnp.einsum('nd,od->no', c, c_weight)
        out = out + ctx[:, :, None] + bias[None, :, None]
        return out

    def _L2_cond_ref(x, embedding, W0, b0, W1, b1, W2, b2, weight, bias_k):
        import jax, jax.numpy as jnp
        import numpy as np
        K = 8
        T = 1.0
        D_EMBD = 128
        IN_C = 128
        OUT_C = 128
        BS = 32
        H = 2048
        HID = 128
        h = jax.nn.gelu(embedding @ W0 + b0, approximate=False)
        h = jax.nn.gelu(h @ W1 + b1, approximate=False)
        att = jax.nn.softmax((h @ W2 + b2) / T, axis=-1)
        agg_w = jnp.einsum('bk,koi->boi', att, weight[..., 0])
        agg_b = att @ bias_k
        out = jnp.einsum('boi,bih->boh', agg_w, x) + agg_b[:, :, None]
        return out

    def _L3_cond_ref(x, c, weight, c_weight, bias):
        import jax, jax.numpy as jnp
        import numpy as np
        from jax import lax
        N, C_IN, L = (32, 128, 2048)
        C_OUT, K, GROUPS = (128, 9, 4)
        C_DIM, PAD, STRIDE = (128, 4, 1)
        out = lax.conv_general_dilated(x, weight, window_strides=(STRIDE,), padding=[(PAD, PAD)], dimension_numbers=('NCH', 'OIH', 'NCH'), feature_group_count=GROUPS)
        ctx = jnp.einsum('nd,od->no', c, c_weight)
        out = out + ctx[:, :, None] + bias[None, :, None]
        return out
    x = x + _L0_cond_ref(x, cond_128, L0_cond_W0, L0_cond_b0, L0_cond_W1, L0_cond_b1, L0_cond_W2, L0_cond_b2, L0_cond_weight, L0_cond_bias_k)
    x = x + _L1_cond_ref(x, cond_128, L1_cond_weight, L1_cond_c_weight, fside_S_0)
    x = x + _L2_cond_ref(x, cond_128, L2_cond_W0, L2_cond_b0, L2_cond_W1, L2_cond_b1, L2_cond_W2, L2_cond_b2, L2_cond_weight, L2_cond_bias_k)
    x = x + _L3_cond_ref(x, cond_128, L3_cond_weight, L3_cond_c_weight, fside_S_0)
    return x

_drawn_inputs = setup_inputs


def setup_inputs(seed=0):
    import zlib

    import numpy as np

    out = dict(_drawn_inputs(seed))
    spreads = {'L0_cond_b0': (0.0, 0.762),
     'L0_cond_b1': (0.0, 0.431),
     'L0_cond_b2': (0.0, 0.413),
     'L2_cond_b0': (0.0, 0.591),
     'L2_cond_b1': (0.0, 0.324),
     'L2_cond_b2': (0.0, 0.396)}
    factors = {'L2_cond_bias_k': 36.347}
    for name, (base, spread) in spreads.items():
        noise = np.random.default_rng([zlib.crc32(name.encode()), seed]).standard_normal(out[name].shape)
        drawn = base * np.exp(spread * noise) if base else spread * noise
        out[name] = jnp.asarray(drawn.astype(out[name].dtype))
    for name, factor in factors.items():
        out[name] = (out[name] * factor).astype(out[name].dtype)
    return out
```

```python
import concourse.bass as bass
from concourse import mybir
from contextlib import ExitStack


def build_cond_resid(nc, x, emb_t, mlp_w, mlp_b, w2_in, b2_in, mix_w, mix_b, conv_w, ctx_w, side, consts, scratch, out):
    fp32 = mybir.dt.float32
    f32r = mybir.dt.float32r
    ALU = mybir.AluOpType
    ACT = mybir.ActivationFunctionType
    AX_X = mybir.AxisListType.X

    B, C, T = x.shape
    PH = 4
    G = 4
    CG = C // G
    N = T // PH
    OFF = 3
    K = mix_b.shape[0]
    NL = 4
    Q = 4
    QW = C * C // Q
    QB = QW // N
    HALO = N + 2
    ROWS = B + 2
    NB = NL * G
    LOADS = 9

    ctx = ExitStack()
    with ctx:
        def sb(name, shape, dt=fp32):
            return ctx.enter_context(nc.sbuf_tensor(name, shape, dt))

        def sem(name):
            return ctx.enter_context(nc.semaphore(name))

        emb_sb = sb("emb_sb", [128, B])
        mlp_w_sb = sb("mlp_w_sb", [128, 4, 128])
        mlp_b_sb = sb("mlp_b_sb", [128, 4])
        w2_sb = sb("w2_sb", [128, 2, K])
        b2_sb = sb("b2_sb", [128, 2, K])
        mix_b_sb = sb("mix_b_sb", [K, 2, G, 128])
        ctx_w_sb = sb("ctx_w_sb", [128, 2, G, 128])
        side_sb = sb("side_sb", [128, G])
        consts_sb = sb("consts_sb", [128, 134])
        ident = consts_sb[:, 0:128]
        w_low = consts_sb[:, 128:129]
        a_low = consts_sb[:, 129:130]
        in_quarter = consts_sb[:, 130:134]
        hidden0 = sb("hidden0", [128, 2, B])
        hidden1 = sb("hidden1", [128, 2, B])
        logits = sb("logits", [128, 2, K])
        top = sb("top", [128, 2])
        neg_max = sb("neg_max", [128, 2])
        expo = sb("expo", [128, 2, K])
        total = sb("total", [128, 2])
        inv = sb("inv", [128, 2])
        att_rep = sb("att_rep", [128, 2, 128])
        att_t = sb("att_t", [128, 2, B])
        att_high = sb("att_high", [128, 2, B], f32r)
        att_parts = sb("att_parts", [128, 2, B], f32r)
        att_q = sb("att_q", [128, 2, Q, B], f32r)
        mix_raw = sb("mix_raw", [128, QW])
        mix_high = sb("mix_high", [128, QW], f32r)
        mix_parts = sb("mix_parts", [128, QW], f32r)
        stage = sb("stage", [128, 2, QW])
        bias_table = sb("bias_table", [128, ROWS, NB])
        conv_raw = sb("conv_raw", [128, G * OFF * 128])
        conv_high = [sb(f"conv_high{i}", [128, G, OFF, 128], f32r) for i in range(2)]
        conv_low = [sb(f"conv_low{i}", [128, G, OFF, 128], f32r) for i in range(2)]

        x_sb = [sb(f"x_sb{s}", [128, T]) for s in range(2)]
        m0_sb = [sb(f"m0_sb{s}", [128, C]) for s in range(2)]
        m2_sb = [sb(f"m2_sb{s}", [128, C]) for s in range(2)]
        bias = [sb(f"bias{s}", [128, NB]) for s in range(2)]
        high = [sb(f"high{i}", [128, G, HALO], f32r) for i in range(2)]
        low = [sb(f"low{i}", [128, G, HALO], f32r) for i in range(2)]
        chan = sb("chan", [128, PH, N])
        out_sb = [stage[:, s, 0:T] for s in range(2)]
        ps = ctx.enter_context(nc.psum_tensor("ps", [128, 8, N], fp32))

        small_in = sem("small_in")
        mix_in = sem("mix_in")
        conv_in = sem("conv_in")
        hid0_mm, ctx_mm, hid1_mm = sem("hid0_mm"), sem("ctx_mm"), sem("hid1_mm")
        logit_mm, att_t_mm, mix_b_mm = sem("logit_mm"), sem("att_t_mm"), sem("mix_b_mm")
        agg_mm = sem("agg_mm")
        hid0_set, hid1_set, expo_set = sem("hid0_set"), sem("hid1_set"), sem("expo_set")
        mix_high_set, conv_high_set = sem("mix_high_set"), sem("conv_high_set")
        agg_act = sem("agg_act")
        dve_chain = sem("dve_chain")
        logits_set, ctx_read, att_set = sem("logits_set"), sem("ctx_read"), sem("att_set")
        att_t_set, att_q_set, mix_b_read = sem("att_t_set"), sem("att_q_set"), sem("mix_b_read")
        mix_set, conv_ident_set, conv_set = sem("mix_set"), sem("conv_ident_set"), sem("conv_set")
        agg_dve = sem("agg_dve")
        agg_set = sem("agg_set")
        zeros_set = sem("zeros_set")
        stored = [sem(f"stored{s}") for s in range(2)]

        x_in = [sem(f"x_in{s}") for s in range(2)]
        m0_in = [sem(f"m0_in{s}") for s in range(2)]
        m2_in = [sem(f"m2_in{s}") for s in range(2)]
        out_done = [sem(f"out_done{s}") for s in range(2)]
        bias_set = sem("bias_set")
        mm = [sem(f"mm_l{i}") for i in range(NL)]
        split_high = [sem("high_l0"), sem("high_l2")]
        split_low = [sem("low_l0"), sem("low_l2")]
        back_act = {1: sem("back_act_l1"), 3: sem("back_act_l3")}
        back_dve = {1: sem("back_dve_l1"), 3: sem("back_dve_l3")}

        ACT_GROUPS, DVE_GROUPS = (0, 2), (1, 3)

        def bias_col(s, layer, g, p0=0, p1=128):
            return bias[s][p0:p1, layer * G + g:layer * G + g + 1]

        def phases(tile):
            return tile.rearrange("c (n p) -> c p n", p=PH)

        def uses(j, s):
            return 8 * j + 16 - 8 * s

        def steps(engine, step, last=B + 2, depth=0):
            for i in range(4):
                step(i, i % 2, False)
            with engine.Fori(2, (B - depth) // 2) as pair:
                step(2 * pair, 0, True)
                step(2 * pair + 1, 1, True)
            for i in range(B - depth, last):
                step(i, i % 2, False)

        def has(i, inner, lag):
            return inner or 0 <= i - lag < B

        block = ctx.enter_context(nc.Block())

        @block.sync
        def _(sp):
            small = ((emb_sb[:], emb_t), (mlp_w_sb[:], mlp_w), (mlp_b_sb[:], mlp_b), (w2_sb[:], w2_in),
                     (b2_sb[:], b2_in), (mix_b_sb[:], mix_b), (ctx_w_sb[:], ctx_w), (side_sb[:], side),
                     (consts_sb[:], consts))
            assert len(small) == LOADS
            for dst, src in small:
                sp.dma_start(dst, src).then_inc(small_in, 16)
            sp.dma_start(mix_raw[:], mix_w[0]).then_inc(mix_in, 16)
            sp.dma_start(conv_raw[:], conv_w[0]).then_inc(conv_in, 16)
            for s in range(2):
                sp.dma_start(x_sb[s][:], x[s]).then_inc(x_in[s], 16)
            sp.wait_ge(mix_set, 1)
            sp.dma_start(mix_raw[:], mix_w[1]).then_inc(mix_in, 16)
            sp.wait_ge(conv_set, 1)
            sp.dma_start(conv_raw[:], conv_w[1]).then_inc(conv_in, 16)

            def store_quarter(n):
                sp.wait_ge(agg_set, n + 1)
                sp.dma_start(scratch[n // Q][:, n % Q * QW:(n % Q + 1) * QW], stage[:, n % 2, :]).then_inc(stored[n % 2], 16)

            def load_matrix(tile, l, b, arrived):
                sp.dma_start(tile[:], scratch[l][b].rearrange("(i o) -> i o", i=C)).then_inc(arrived, 16)

            for n in range(Q + 1):
                store_quarter(n)
            for s in range(2):
                sp.wait_ge(stored[s], 16 * (Q // 2))
            for s in range(2):
                load_matrix(m0_sb[s], 0, s, m0_in[s])
            for n in range(Q + 1, 2 * Q):
                store_quarter(n)
            for s in range(2):
                sp.wait_ge(stored[s], 16 * Q)
            for s in range(2):
                load_matrix(m2_sb[s], 1, s, m2_in[s])

            def step(i, s, inner):
                if inner or i + 2 < B:
                    sp.wait_ge(mm[0], G * i + G)
                    sp.dma_start(x_sb[s][:], x[i + 2]).then_inc(x_in[s], 16)
                    load_matrix(m0_sb[s], 0, i + 2, m0_in[s])
                if has(i, inner, 2):
                    sp.wait_ge(back_act[3], 2 * (i - 2) + 2)
                    sp.wait_ge(back_dve[3], 2 * (i - 2) + 2)
                    sp.dma_start(out[i - 2], out_sb[s]).then_inc(out_done[s], 16)
                if inner or (i >= 1 and i + 1 < B):
                    sp.wait_ge(mm[2], G * (i - 1) + G)
                    load_matrix(m2_sb[1 - s], 1, i + 1, m2_in[1 - s])

            steps(sp, step, depth=2)
            for s in range(2):
                sp.wait_ge(out_done[s], 16 * (B // 2))

        @block.tensor
        def _(pe):
            pe.wait_ge(small_in, 16 * LOADS)
            for l in range(2):
                nc.tensor.matmul(ps[:, l, 0:B], mlp_w_sb[:, 2 * l, :], emb_sb[:], start=True, stop=True).then_inc(hid0_mm, 1)
            for l in range(2):
                for g in range(G):
                    last = nc.tensor.matmul(ps[:, 2 + l, g * B:(g + 1) * B], ctx_w_sb[:, l, g, :], emb_sb[:], start=True, stop=True)
                last.then_inc(ctx_mm, 1)
            for l in range(2):
                pe.wait_ge(hid0_set, l + 1)
                nc.tensor.matmul(ps[:, 4 + l, 0:B], mlp_w_sb[:, 2 * l + 1, :], hidden0[:, l, :], start=True, stop=True).then_inc(hid1_mm, 1)
            for l in range(2):
                pe.wait_ge(hid1_set, l + 1)
                nc.tensor.matmul(ps[:, 6 + l, 0:K], hidden1[:, l, :], w2_sb[:, l, :], start=True, stop=True).then_inc(logit_mm, 1)
            for l in range(2):
                pe.wait_ge(att_set, l + 1)
                nc.tensor.matmul(ps[:, l, 0:B], att_rep[:, l, :], ident, start=True, stop=True).then_inc(att_t_mm, 1)
            for l in range(2):
                pe.wait_ge(att_t_set, l + 1)
                for g in range(G):
                    last = nc.tensor.matmul(ps[:, 4 + l, g * B:(g + 1) * B], mix_b_sb[:, l, g, :], att_t[0:K, l, :], start=True, stop=True)
                last.then_inc(mix_b_mm, 1)
            pe.wait_ge(att_q_set, 1)
            pe.wait_ge(ctx_read, 2)
            pe.wait_ge(mix_b_read, 2)
            for n in range(2 * Q):
                pe.wait_ge(mix_set, n // Q + 1)
                for m in range(QB):
                    if n > 0:
                        pe.wait_ge((agg_act, agg_dve)[m % 2], (n - 1) * (QB // 2) + m // 2 + 1)
                    nc.tensor.matmul(ps[:, m, :], att_q[:, n // Q, n % Q, :], mix_parts[:, m * N:(m + 1) * N],
                                     start=True, stop=True).then_inc(agg_mm, 1)
            pe.wait_ge(conv_set, 2)
            pe.wait_ge(zeros_set, 1)
            pe.wait_ge(agg_act, Q * QB)
            pe.wait_ge(agg_dve, Q * QB)

            def pointwise(layer, g, mat, moving):
                for p in range(PH):
                    last = nc.tensor.matmul(ps[CG * p:CG * (p + 1), g, :], mat[:, CG * g:CG * (g + 1)], moving[:, p, :],
                                            start=True, stop=True)
                last.then_inc(mm[layer], 1)

            def convolution(layer, g):
                c = layer // 2
                passes = [(w, a, o) for o in range(OFF) for w, a in
                          ((conv_high[c], high[c]), (conv_high[c], low[c]), (conv_low[c], high[c]))]
                for n, (w, a, o) in enumerate(passes):
                    last = nc.tensor.matmul(ps[:, 4 + g, :], w[:, g, o, :], a[:, g, o:o + N],
                                            start=(n == 0), stop=(n == len(passes) - 1))
                last.then_inc(mm[layer], 1)

            def wait_back(layer, j, g):
                pe.wait_ge((back_act if g in ACT_GROUPS else back_dve)[layer], 2 * j + g // 2 + 1)

            def step(i, s, inner):
                if has(i, inner, 0):
                    pe.wait_ge(x_in[s], uses(i, s))
                    pe.wait_ge(m0_in[s], uses(i, s))
                    for g in range(G):
                        if has(i, inner, 2):
                            pe.wait_ge(split_low[1], G * (i - 2) + g + 1)
                        elif i >= 1:
                            pe.wait_ge(split_low[0], G * (i - 1) + g + 1)
                        pointwise(0, g, m0_sb[s], phases(x_sb[s][:]))
                if has(i, inner, 2):
                    for g in range(G):
                        pe.wait_ge(split_low[1], G * (i - 2) + g + 1)
                        if has(i, inner, 1):
                            wait_back(1, i - 1, g)
                        else:
                            wait_back(3, i - 3, g)
                        convolution(3, g)
                if has(i, inner, 1):
                    pe.wait_ge(m2_in[1 - s], uses(i - 1, 1 - s))
                    pe.wait_ge(back_act[1], 2 * (i - 1) + 2)
                    pe.wait_ge(back_dve[1], 2 * (i - 1) + 2)
                    for g in range(G):
                        if has(i, inner, 0):
                            pe.wait_ge(split_low[0], G * i + g + 1)
                        else:
                            pe.wait_ge(split_low[1], G * (i - 2) + g + 1)
                        pointwise(2, g, m2_sb[1 - s], chan)
                if has(i, inner, 0):
                    for g in range(G):
                        pe.wait_ge(split_low[0], G * i + g + 1)
                        if has(i, inner, 2):
                            wait_back(3, i - 2, g)
                        elif i >= 1:
                            wait_back(1, i - 1, g)
                        convolution(1, g)

            steps(pe, step)

        @block.scalar
        def _(act):
            act.wait_ge(small_in, 16 * LOADS)
            for l in range(2):
                act.wait_ge(hid0_mm, l + 1)
                nc.scalar.activation(hidden0[:, l, :], ps[:, l, 0:B], ACT.Gelu, bias=mlp_b_sb[:, 2 * l:2 * l + 1]).then_inc(hid0_set, 1)
            for l in range(2):
                act.wait_ge(hid1_mm, l + 1)
                nc.scalar.activation(hidden1[:, l, :], ps[:, 4 + l, 0:B], ACT.Gelu,
                                     bias=mlp_b_sb[:, 2 * l + 1:2 * l + 2]).then_inc(hid1_set, 1)
            for l in range(2):
                act.wait_ge(logits_set, l + 1)
                nc.scalar.activation(expo[:, l, :], logits[:, l, :], ACT.Exp, bias=neg_max[:, l:l + 1],
                                     accum_out=total[:, l:l + 1]).then_inc(expo_set, 1)
            for l in range(2):
                act.wait_ge(mix_in, 16 * (l + 1))
                if l:
                    act.wait_ge(mix_set, l)
                nc.scalar.copy(mix_high[:], mix_raw[:]).then_inc(mix_high_set, 1)
                act.wait_ge(conv_ident_set, l + 1)
                nc.scalar.copy(conv_high[l][:].rearrange("p g o m -> p (g o m)"), conv_raw[:]).then_inc(conv_high_set, 1)
                for n in range(l * Q, (l + 1) * Q):
                    if n >= 2:
                        act.wait_ge(stored[n % 2], 16 * (n // 2))
                    for m in range(0, QB, 2):
                        act.wait_ge(agg_mm, n * QB + m + 1)
                        nc.scalar.copy(stage[:, n % 2, m * N:(m + 1) * N], ps[:, m, :]).then_inc(agg_act, 1)

            def high_parts(l, j, s):
                for g in range(G):
                    act.wait_ge(mm[2 * l], G * j + g + 1)
                    nc.scalar.activation(high[l][:, g, 1:N + 1], ps[:, g, :], ACT.Identity,
                                         bias=bias_col(s, 2 * l, g)).then_inc(split_high[l], 1)

            def back(layer, j, s, dst):
                for g in ACT_GROUPS:
                    act.wait_ge(mm[layer], G * j + g + 1)
                    for p in range(PH):
                        last = nc.scalar.activation(dst[CG * g:CG * (g + 1), p, :], ps[CG * p:CG * (p + 1), 4 + g, :],
                                                    ACT.Identity, bias=bias_col(s, layer, g, CG * p, CG * (p + 1)))
                    last.then_inc(back_act[layer], 1)

            def step(i, s, inner):
                act.wait_ge(bias_set, i + 1)
                if has(i, inner, 0):
                    high_parts(0, i, s)
                if has(i, inner, 2):
                    if has(i, inner, 4):
                        act.wait_ge(out_done[s], uses(i - 4, s))
                    back(3, i - 2, s, phases(out_sb[s]))
                if has(i, inner, 1):
                    high_parts(1, i - 1, s)
                if has(i, inner, 0):
                    back(1, i, s, chan)

            steps(act, step)

        @block.vector
        def _(dve):
            chained = [0]

            def chain(ins):
                chained[0] += 1
                ins.then_inc(dve_chain, 1)
                dve.wait_ge(dve_chain, chained[0])

            def table(layer, g):
                lag = (0, 0, 1, 2)[layer]
                return bias_table[:, lag:lag + B, layer * G + g]

            for t in (*high, *low):
                last = nc.vector.memset(t[:, :, 0:HALO:HALO - 1].bitcast(fp32), 0.0)
            last.then_inc(zeros_set, 1)
            chain(nc.vector.memset(bias_table[:], 0.0))
            dve.wait_ge(small_in, 16 * LOADS)
            conv_raw_v = conv_raw[:].rearrange("p (g o m) -> p g o m", g=G, o=OFF)

            def conv_identity(l):
                dve.wait_ge(conv_in, 16 * (l + 1))
                for g in range(G):
                    last = nc.vector.tensor_tensor(conv_raw_v[:, g, 1, :], conv_raw_v[:, g, 1, :], ident, ALU.add)
                last.then_inc(conv_ident_set, 1)

            for l in range(2):
                dve.wait_ge(ctx_mm, l + 1)
                for g in range(G):
                    last = nc.vector.tensor_scalar(table(2 * l + 1, g), ps[:, 2 + l, g * B:(g + 1) * B], side_sb[:, g:g + 1], None, ALU.add)
                last.then_inc(ctx_read, 1)
            for l in range(2):
                dve.wait_ge(logit_mm, l + 1)
                chain(nc.vector.tensor_tensor(logits[:, l, :], ps[:, 6 + l, 0:K], b2_sb[:, l, :], ALU.add))
                chain(nc.vector.reduce_max(top[:, l:l + 1], logits[:, l, :], AX_X))
                nc.vector.tensor_scalar(neg_max[:, l:l + 1], top[:, l:l + 1], -1.0, None, ALU.mult).then_inc(logits_set, 1)
            for l in range(2):
                dve.wait_ge(expo_set, l + 1)
                chain(nc.vector.reciprocal(inv[:, l:l + 1], total[:, l:l + 1]))
                chain(nc.vector.tensor_scalar(att_rep[:, l, 0:K], expo[:, l, :], inv[:, l:l + 1], None, ALU.mult))
                width = K
                while width < 128:
                    ins = nc.vector.tensor_copy(att_rep[:, l, width:2 * width], att_rep[:, l, 0:width])
                    width *= 2
                    if width < 128:
                        chain(ins)
                ins.then_inc(att_set, 1)
            for l in range(2):
                dve.wait_ge(att_t_mm, l + 1)
                nc.vector.tensor_copy(att_t[:, l, :], ps[:, l, 0:B]).then_inc(att_t_set, 1)
            dve.wait_ge(att_t_set, 2)
            chain(nc.vector.tensor_copy(att_high[:], att_t[:]))
            chain(nc.vector.scalar_tensor_tensor(out=att_parts[:], in0=att_high[:].bitcast(fp32), scalar=a_low, in1=att_t[:],
                                                 op0=ALU.mult, op1=ALU.add))
            for q in range(Q):
                last = nc.vector.tensor_scalar(att_q[:, :, q, :], att_parts[:].bitcast(fp32), in_quarter[:, q:q + 1], None, ALU.mult)
            last.then_inc(att_q_set, 1)
            for l in range(2):
                dve.wait_ge(mix_b_mm, l + 1)
                for g in range(G):
                    last = nc.vector.tensor_copy(table(2 * l, g), ps[:, 4 + l, g * B:(g + 1) * B])
                last.then_inc(mix_b_read, 1)

            for l in range(2):
                dve.wait_ge(mix_high_set, l + 1)
                if l:
                    dve.wait_ge(agg_mm, Q * QB)
                nc.vector.scalar_tensor_tensor(out=mix_parts[:], in0=mix_high[:].bitcast(fp32), scalar=w_low, in1=mix_raw[:],
                                               op0=ALU.mult, op1=ALU.add).then_inc(mix_set, 1)
                conv_identity(l)
                dve.wait_ge(conv_high_set, l + 1)
                nc.vector.tensor_tensor(conv_low[l][:].rearrange("p g o m -> p (g o m)"), conv_raw[:],
                                        conv_high[l][:].bitcast(fp32).rearrange("p g o m -> p (g o m)"),
                                        ALU.subtract).then_inc(conv_set, 1)
                for n in range(l * Q, (l + 1) * Q):
                    if n >= 2:
                        dve.wait_ge(stored[n % 2], 16 * (n // 2))
                    for m in range(1, QB, 2):
                        dve.wait_ge(agg_mm, n * QB + m + 1)
                        nc.vector.tensor_copy(stage[:, n % 2, m * N:(m + 1) * N], ps[:, m, :]).then_inc(agg_dve, 1)
                    dve.wait_ge(agg_act, (n + 1) * (QB // 2))
                    dve.wait_ge(agg_dve, (n + 1) * (QB // 2))
                    first = n % Q * (C // Q)
                    diagonal = stage[:, n % 2, first:first + (C + 1) * (C // Q - 1) + 1:C + 1]
                    nc.vector.tensor_scalar(diagonal, diagonal, 1.0, None, ALU.add).then_inc(agg_set, 1)

            def low_parts(l, j, s):
                for g in range(G):
                    dve.wait_ge(split_high[l], G * j + g + 1)
                    nc.vector.scalar_tensor_tensor(out=low[l][:, g, 1:N + 1], in0=ps[:, g, :], scalar=bias_col(s, 2 * l, g),
                                                   in1=high[l][:, g, 1:N + 1].bitcast(fp32),
                                                   op0=ALU.add, op1=ALU.subtract).then_inc(split_low[l], 1)

            def back(layer, j, s, dst):
                for g in DVE_GROUPS:
                    dve.wait_ge(mm[layer], G * j + g + 1)
                    for p in range(PH):
                        last = nc.vector.tensor_scalar(dst[CG * g:CG * (g + 1), p, :], ps[CG * p:CG * (p + 1), 4 + g, :],
                                                       bias_col(s, layer, g, CG * p, CG * (p + 1)), None, ALU.add)
                    last.then_inc(back_dve[layer], 1)

            def step(i, s, inner):
                dve.wait_ge(bias_set, i + 1)
                if has(i, inner, 0):
                    low_parts(0, i, s)
                if has(i, inner, 2):
                    if has(i, inner, 4):
                        dve.wait_ge(out_done[s], uses(i - 4, s))
                    back(3, i - 2, s, phases(out_sb[s]))
                if has(i, inner, 1):
                    low_parts(1, i - 1, s)
                if has(i, inner, 0):
                    back(1, i, s, chan)

            steps(dve, step)

        @block.gpsimd
        def _(pool):
            pool.wait_ge(mix_b_read, 2)

            def step(i, s, inner):
                if inner or i >= 2:
                    pool.wait_ge(back_act[1], 2 * (i - 2) + 2)
                    pool.wait_ge(back_dve[1], 2 * (i - 2) + 2)
                nc.gpsimd.tensor_copy(bias[s][:], bias_table[:, i, :]).then_inc(bias_set, 1)

            steps(pool, step)


def kernel(x, cond_128, fside_S_0, **weights):
    import numpy as np
    import concourse.bacc as bacc
    from concourse.bass_utils import run_bass_kernel_spmd

    dense, conv = ("L0_cond_", "L2_cond_"), ("L1_cond_", "L3_cond_")
    w = {name: np.asarray(a) for name, a in weights.items()}
    x, cond, side = np.asarray(x), np.asarray(cond_128), np.asarray(fside_S_0)
    B, C, T = x.shape
    K = w["L0_cond_bias_k"].shape[0]
    G, PH, OFF, Q = 4, 4, 3, 4
    CG = C // G
    TAPS = w["L1_cond_weight"].shape[2]
    HALF = TAPS // 2

    def by_phases(a):
        a = a.reshape(*a.shape[:-1], G, 1, CG)
        return np.broadcast_to(a, (*a.shape[:-2], PH, CG)).reshape(*a.shape[:-2], PH * CG)

    def toeplitz(taps):
        t = np.zeros((PH, CG, G, OFF, PH, CG), taps.dtype)
        v = taps.reshape(G, CG, CG, TAPS)
        for p_in in range(PH):
            for o in range(OFF):
                for p_out in range(PH):
                    tap = PH * (o - 1) + p_in - p_out + HALF
                    if 0 <= tap < TAPS:
                        t[p_in, :, :, o, p_out, :] = v[:, :, :, tap].transpose(2, 0, 1)
        return t.reshape(PH * CG, G * OFF * PH * CG)

    part = np.arange(128)
    copy = part % 32 // K
    consts = np.zeros((128, 134), np.float32)
    consts[:, 0:128] = np.eye(128)
    consts[:, 128] = np.where(copy >= 2, -1, 0)
    consts[:, 129] = -(copy % 2)
    consts[:, 130:134] = part[:, None] // 32 == np.arange(Q)

    def mixing(a):
        a = a[..., 0].transpose(0, 2, 1).reshape(K, Q, 1, C * C // Q).transpose(1, 2, 0, 3)
        return np.broadcast_to(a, (Q, 32 // K, K, C * C // Q)).reshape(128, C * C // Q)

    arrays = {
        "x": x,
        "emb_t": cond.T,
        "mlp_w": np.stack([w[p + n] for p in dense for n in ("W0", "W1")], axis=1),
        "mlp_b": np.stack([w[p + n] for p in dense for n in ("b0", "b1")], axis=1),
        "w2_in": np.stack([w[p + "W2"] for p in dense], axis=1),
        "b2_in": np.broadcast_to(np.stack([w[p + "b2"] for p in dense]), (128, 2, K)),
        "mix_w": np.stack([mixing(w[p + "weight"]) for p in dense]),
        "mix_b": np.stack([by_phases(w[p + "bias_k"]) for p in dense], axis=1),
        "conv_w": np.stack([toeplitz(w[p + "weight"]) for p in conv]),
        "ctx_w": np.stack([by_phases(w[p + "c_weight"].T) for p in conv], axis=1),
        "side": by_phases(side).T,
        "consts": consts,
    }
    arrays = {name: np.ascontiguousarray(a) for name, a in arrays.items()}
    nc = bacc.Bacc("TRN2", target_bir_lowering=False, num_devices=1)
    aps = {name: nc.dram_tensor(name, a.shape, mybir.dt.from_np(a.dtype), kind="ExternalInput").ap()
           for name, a in arrays.items()}
    scratch = nc.dram_tensor("mixed", (2, B, C * C), mybir.dt.float32, kind="Internal").ap()
    out = nc.dram_tensor("out", (B, C, T), mybir.dt.float32, kind="ExternalOutput").ap()
    build_cond_resid(nc, scratch=scratch, out=out, **aps)
    r = run_bass_kernel_spmd(nc, [arrays], core_ids=[0])
    return r.results[0]["out"]
```

```python
import concourse.bass as bass
from concourse import mybir
from contextlib import ExitStack


def build_cond_resid(nc, x, emb_t, mlp_w, mlp_b, w2_in, b2_in, mix_w, mix_b, conv_w, ctx_w, side, consts, scratch, out):
    fp32 = mybir.dt.float32
    f32r = mybir.dt.float32r
    ALU = mybir.AluOpType
    ACT = mybir.ActivationFunctionType
    AX_X = mybir.AxisListType.X

    B, C, T = x.shape
    PAIRS = B // 2
    PH = 4
    G = 4
    CG = C // G
    N = T // PH
    OFF = 3
    K = mix_b.shape[0]
    NL = 4
    Q = 4
    QW = C * C // Q
    QB = QW // N
    HALO = N + 2
    HIGH, LOW = 0, 1
    LOADS = 9

    ctx = ExitStack()
    with ctx:
        def sb(name, shape, dt=fp32):
            return ctx.enter_context(nc.sbuf_tensor(name, shape, dt))

        def sem(name):
            return ctx.enter_context(nc.semaphore(name))

        x_t = sb("x_t", [128, 2, T])
        pw = sb("pw", [128, 2, 2, PH, N], f32r)
        cv = sb("cv", [128, 2, 2, G, HALO], f32r)
        chan = sb("chan", [128, 2, PH, N])
        chan_out = sb("chan_out", [128, PH, 2, N])
        ph_in = {1: sb("ph_in1", [128, G, 2, N]), 3: sb("ph_in3", [128, G, 2, N])}
        out_t = sb("out_t", [128, 2, T])
        m_raw = {l: sb(f"m_raw{l}", [128, 2, C]) for l in (0, 2)}
        m_parts = {l: sb(f"m_parts{l}", [128, 2, 2, C], f32r) for l in (0, 2)}
        bias = [sb(f"bias{l}", [128, 2, G]) for l in range(NL)]
        conv_parts = {l: sb(f"conv_parts{l}", [128, 2, G, OFF, 128], f32r) for l in (1, 3)}
        bias_table = sb("bias_table", [128, B, NL * G])
        ps = ctx.enter_context(nc.psum_tensor("ps", [128, 8, N], fp32))

        conv_raw = sb("conv_raw", [128, G * OFF * 128])
        consts_sb = sb("consts_sb", [128, 134])
        ident = consts_sb[:, 0:128]
        w_low = consts_sb[:, 128:129]
        a_low = consts_sb[:, 129:130]
        in_quarter = consts_sb[:, 130:134]
        small_sb = sb("small_sb", [128, 64])

        def flat(tile, pattern):
            return tile[:].rearrange(f"lane {pattern} -> lane ({pattern})")

        mix_raw = flat(x_t, "s t")
        mix_high = flat(pw, "s r p n")[:, 0:QW]
        mix_parts = flat(cv, "s r g n")[:, 0:QW]
        room_r = flat(cv, "s r g n")[:, QW:]
        stage = [flat(chan_out, "p s n"), flat(out_t, "s t"), flat(ph_in[1], "g s n"), flat(ph_in[3], "g s n")]
        room = flat(chan, "s p n")
        taken = {id(room): 0, id(room_r): 0, id(small_sb): 0}

        def part_of(where, tile, shape, pattern=None):
            width = 1
            for n in shape[1:]:
                width *= n
            first = taken[id(where)]
            taken[id(where)] += width
            view = tile[0:shape[0], first:first + width]
            names = "abcd"[:len(shape) - 1]
            return view if len(shape) == 2 else view.rearrange(
                f"p ({' '.join(names)}) -> p {' '.join(names)}", **dict(zip(names, shape[1:])))

        emb_sb = part_of(room, room, [128, B])
        mlp_w_sb = part_of(room, room, [128, 4, 128])
        mix_b_sb = part_of(room, room, [K, 2, 128])
        ctx_w_sb = part_of(room, room, [128, 2, G, 128])
        hidden0 = part_of(room, room, [128, 2, B])
        hidden1 = part_of(room, room, [128, 2, B])
        att_rep = part_of(room, room, [128, 2, 128])
        att_t = part_of(room, room, [128, 2, B])
        att_high = part_of(room_r, room_r, [128, 2, B])
        att_parts = part_of(room_r, room_r, [128, 2, B])
        att_q = part_of(room_r, room_r, [128, 2, Q, B])
        small = small_sb[:]
        mlp_b_sb = part_of(small_sb, small, [128, 4])
        w2_sb = part_of(small_sb, small, [128, 2, K])
        b2_sb = part_of(small_sb, small, [128, 2, K])
        side_sb = part_of(small_sb, small, [128, G])
        logits = sb("logits", [128, 2, K])
        expo = sb("expo", [128, 2, K])
        top, neg_max, total, inv = (sb(n, [128, 2]) for n in ("top", "neg_max", "total", "inv"))

        small_in = sem("small_in")
        mix_in = sem("mix_in")
        conv_in = sem("conv_in")
        hid0_mm, ctx_mm, hid1_mm = sem("hid0_mm"), sem("ctx_mm"), sem("hid1_mm")
        logit_mm, att_t_mm, mix_b_mm = sem("logit_mm"), sem("att_t_mm"), sem("mix_b_mm")
        agg_mm = sem("agg_mm")
        hid0_set, hid1_set, expo_set = sem("hid0_set"), sem("hid1_set"), sem("expo_set")
        mix_high_set, conv_high_set = sem("mix_high_set"), sem("conv_high_set")
        agg_act = sem("agg_act")
        dve_chain = sem("dve_chain")
        logits_set, ctx_read, att_set = sem("logits_set"), sem("ctx_read"), sem("att_set")
        att_t_set, att_q_set, mix_b_read = sem("att_t_set"), sem("att_q_set"), sem("mix_b_read")
        mix_set, conv_ident_set, conv_set = sem("mix_set"), sem("conv_ident_set"), sem("conv_set")
        agg_dve = sem("agg_dve")
        agg_set = sem("agg_set")
        zeros_set = sem("zeros_set")
        stored = [sem(f"stored{s}") for s in range(Q)]

        x_in = [sem(f"x_in{s}") for s in range(2)]
        m_in = {l: sem(f"m_in{l}") for l in (0, 2)}
        ph_moved = {l: [sem(f"ph_moved{l}_{g}") for g in range(G)] for l in (1, 3)}
        out_done = [sem(f"out_done{s}") for s in range(2)]
        mm = [sem(f"mm{l}") for l in range(NL)]
        evac = {l: sem(f"evac{l}") for l in (0, 2)}
        back_act = {l: sem(f"back_act{l}") for l in (1, 3)}
        back_dve = {l: sem(f"back_dve{l}") for l in (1, 3)}
        high_set = [[sem(f"high_set{l}_{s}") for s in range(2)] for l in range(NL)]
        low_dve = {l: sem(f"low_dve{l}") for l in (1, 3)}
        low_pool = [sem(f"low_pool{l}") for l in range(NL)]
        m_high_set = {l: sem(f"m_high_set{l}") for l in (0, 2)}
        m_set = {l: sem(f"m_set{l}") for l in (0, 2)}
        bias_set = [sem(f"bias_set{l}") for l in range(NL)]

        BACK_ACT = {1: (0, 2), 3: (0,)}
        BACK_DVE = {1: (1, 3), 3: (1, 2, 3)}
        LOW_DVE = {1: (1, 2, 3), 3: (0, 1, 2)}
        LOW_POOL = {1: (0,), 3: (3,)}

        def nth(j, s, k, mine=(0, 1, 2, 3)):
            return len(mine) * (2 * j + s) + mine.index(k) + 1

        def steps(engine, step):
            for i in range(-1, 3):
                step(i, False)
            with engine.Fori(3, PAIRS - 2) as i:
                step(i, True)
            for i in range(PAIRS - 2, PAIRS + 2):
                step(i, False)

        def has(i, inner, lag):
            return inner or 0 <= i - lag < PAIRS

        def bias_col(layer, s, g, p0=0, p1=128):
            return bias[layer][p0:p1, s, g:g + 1]

        block = ctx.enter_context(nc.Block())

        @block.sync
        def _(sp):
            small_loads = ((emb_sb, emb_t), (mlp_w_sb, mlp_w), (mlp_b_sb, mlp_b), (w2_sb, w2_in), (b2_sb, b2_in),
                           (mix_b_sb, mix_b), (ctx_w_sb, ctx_w), (side_sb, side), (consts_sb[:], consts))
            assert len(small_loads) == LOADS
            for dst, src in small_loads:
                sp.dma_start(dst, src).then_inc(small_in, 16)
            sp.dma_start(mix_raw, mix_w[0]).then_inc(mix_in, 16)
            sp.dma_start(conv_raw[:], conv_w[0]).then_inc(conv_in, 16)
            sp.wait_ge(mix_set, 1)
            sp.dma_start(mix_raw, mix_w[1]).then_inc(mix_in, 16)
            sp.wait_ge(conv_set, 1)
            sp.dma_start(conv_raw[:], conv_w[1]).then_inc(conv_in, 16)

            def store_quarter(n):
                sp.wait_ge(agg_set, n + 1)
                sp.dma_start(scratch[n // Q][:, n % Q * QW:(n % Q + 1) * QW], stage[n % Q]).then_inc(stored[n % Q], 16)

            def load_matrices(l, j):
                sp.dma_start(m_raw[l][:], scratch[l // 2][bass.ds(2 * j, 2)].rearrange("s (i o) -> i s o", i=C)).then_inc(m_in[l], 16)

            def load_x(j, s):
                sp.dma_start(x_t[:, s, :], x[2 * j + s]).then_inc(x_in[s], 16)

            for n in range(Q):
                store_quarter(n)
            sp.wait_ge(mix_set, 2)
            for s in range(2):
                load_x(0, s)
            for q in range(Q):
                sp.wait_ge(stored[q], 16)
            load_matrices(0, 0)
            for n in range(Q, 2 * Q):
                store_quarter(n)
            for q in range(Q):
                sp.wait_ge(stored[q], 32)
            load_matrices(2, 0)

            def to_phases(layer, j):
                for g in range(G):
                    for p in range(PH):
                        if g == 0:
                            sp.wait_ge(evac[layer - 1], nth(j, 1, p))
                        sp.dma_start(ph_in[layer][CG * p:CG * (p + 1), g], chan_out[CG * g:CG * (g + 1), p]).then_inc(ph_moved[layer][g], 16)

            def wait_parts(layer, j):
                sp.wait_ge(low_pool[layer], nth(j, 1, LOW_POOL[layer][-1], LOW_POOL[layer]))
                sp.wait_ge(low_dve[layer], nth(j, 1, LOW_DVE[layer][-1], LOW_DVE[layer]))

            def store_out(j, s):
                sp.wait_ge(back_act[3], nth(j, s, BACK_ACT[3][-1], BACK_ACT[3]))
                sp.wait_ge(back_dve[3], nth(j, s, BACK_DVE[3][-1], BACK_DVE[3]))
                sp.dma_start(out[2 * j + s], out_t[:, s, :]).then_inc(out_done[s], 16)

            def step(i, inner):
                if has(i, inner, 0):
                    if inner or i >= 1:
                        wait_parts(1, i - 1)
                    to_phases(1, i)
                if has(i, inner, 2):
                    store_out(i - 2, 0)
                    store_out(i - 2, 1)
                if has(i, inner, 1):
                    if has(i, inner, 2):
                        wait_parts(3, i - 2)
                    to_phases(3, i - 1)
                if inner or 1 <= i < PAIRS:
                    sp.wait_ge(m_set[2], i)
                    load_matrices(2, i)
                if inner or -1 <= i < PAIRS - 2:
                    sp.wait_ge(m_set[0], i + 2)
                    load_matrices(0, i + 2)
                    for s in range(2):
                        sp.wait_ge(low_pool[0], nth(i + 1, s, PH - 1))
                        load_x(i + 2, s)

            steps(sp, step)
            for s in range(2):
                sp.wait_ge(out_done[s], 16 * PAIRS)

        @block.tensor
        def _(pe):
            pe.wait_ge(small_in, 16 * LOADS)
            for l in range(2):
                nc.tensor.matmul(ps[:, l, 0:B], mlp_w_sb[:, 2 * l, :], emb_sb, start=True, stop=True).then_inc(hid0_mm, 1)
            for l in range(2):
                for g in range(G):
                    last = nc.tensor.matmul(ps[:, 2 + l, g * B:(g + 1) * B], ctx_w_sb[:, l, g, :], emb_sb, start=True, stop=True)
                last.then_inc(ctx_mm, 1)
            for l in range(2):
                pe.wait_ge(hid0_set, l + 1)
                nc.tensor.matmul(ps[:, 4 + l, 0:B], mlp_w_sb[:, 2 * l + 1, :], hidden0[:, l, :], start=True, stop=True).then_inc(hid1_mm, 1)
            for l in range(2):
                pe.wait_ge(hid1_set, l + 1)
                nc.tensor.matmul(ps[:, 6 + l, 0:K], hidden1[:, l, :], w2_sb[:, l, :], start=True, stop=True).then_inc(logit_mm, 1)
            for l in range(2):
                pe.wait_ge(att_set, l + 1)
                nc.tensor.matmul(ps[:, l, 0:B], att_rep[:, l, :], ident, start=True, stop=True).then_inc(att_t_mm, 1)
            for l in range(2):
                pe.wait_ge(att_t_set, l + 1)
                nc.tensor.matmul(ps[:, 4 + l, 0:B], mix_b_sb[:, l, :], att_t[0:K, l, :], start=True, stop=True).then_inc(mix_b_mm, 1)
            pe.wait_ge(att_q_set, 1)
            pe.wait_ge(ctx_read, 2)
            pe.wait_ge(mix_b_read, 2)
            for n in range(2 * Q):
                pe.wait_ge(mix_set, n // Q + 1)
                for m in range(QB):
                    if n > 0:
                        pe.wait_ge((agg_act, agg_dve)[m % 2], (n - 1) * (QB // 2) + m // 2 + 1)
                    nc.tensor.matmul(ps[:, m, :], att_q[:, n // Q, n % Q, :], mix_parts[:, m * N:(m + 1) * N],
                                     start=True, stop=True).then_inc(agg_mm, 1)
            pe.wait_ge(conv_set, 2)
            pe.wait_ge(zeros_set, 1)
            pe.wait_ge(agg_act, Q * QB)
            pe.wait_ge(agg_dve, Q * QB)

            def pointwise(layer, j, s, wait_bank):
                for p in range(PH):
                    pe.wait_ge(low_pool[layer], nth(j, s, p))
                    wait_bank(p)
                    for n, (m, a) in enumerate(((HIGH, HIGH), (HIGH, LOW), (LOW, HIGH))):
                        last = nc.tensor.matmul(ps[:, p, :], m_parts[layer][:, m, s, :], pw[:, s, a, p, :],
                                                start=(n == 0), stop=(n == 2))
                    last.then_inc(mm[layer], 1)

            def convolution(layer, j, s, wait_bank):
                passes = [(w, a, o) for o in range(OFF) for w, a in ((HIGH, HIGH), (HIGH, LOW), (LOW, HIGH))]
                for g in range(G):
                    if g in LOW_DVE[layer]:
                        pe.wait_ge(low_dve[layer], nth(j, s, g, LOW_DVE[layer]))
                    else:
                        pe.wait_ge(low_pool[layer], nth(j, s, g, LOW_POOL[layer]))
                    wait_bank(g)
                    for n, (w, a, o) in enumerate(passes):
                        last = nc.tensor.matmul(ps[:, 4 + g, :], conv_parts[layer][:, w, g, o, :], cv[:, s, a, g, o:o + N],
                                                start=(n == 0), stop=(n == len(passes) - 1))
                    last.then_inc(mm[layer], 1)

            def evacuated(layer, j, s):
                return lambda p: pe.wait_ge(evac[layer], nth(j, s, p))

            def taken_back(layer, j, s):
                def wait(g):
                    if g in BACK_ACT[layer]:
                        pe.wait_ge(back_act[layer], nth(j, s, g, BACK_ACT[layer]))
                    else:
                        pe.wait_ge(back_dve[layer], nth(j, s, g, BACK_DVE[layer]))
                return wait

            def free(k):
                pass

            def step(i, inner):
                now, last, before = has(i, inner, 0), has(i, inner, 1), has(i, inner, 2)
                if now:
                    pe.wait_ge(m_set[0], i + 1)
                    pointwise(0, i, 0, evacuated(2, i - 2, 1) if before else evacuated(0, i - 1, 1) if i else free)
                if before:
                    convolution(3, i - 2, 0, taken_back(1, i - 1, 1) if last else taken_back(3, i - 3, 1))
                if now:
                    pointwise(0, i, 1, evacuated(0, i, 0))
                if before:
                    convolution(3, i - 2, 1, taken_back(3, i - 2, 0))
                if last:
                    pe.wait_ge(m_set[2], i)
                    pointwise(2, i - 1, 0, evacuated(0, i, 1) if now else evacuated(2, i - 2, 1))
                if now:
                    convolution(1, i, 0, taken_back(3, i - 2, 1) if before else taken_back(1, i - 1, 1) if i else free)
                if last:
                    pointwise(2, i - 1, 1, evacuated(2, i - 1, 0))
                if now:
                    convolution(1, i, 1, taken_back(1, i, 0))

            steps(pe, step)

        @block.scalar
        def _(act):
            act.wait_ge(small_in, 16 * LOADS)
            for l in range(2):
                act.wait_ge(hid0_mm, l + 1)
                nc.scalar.activation(hidden0[:, l, :], ps[:, l, 0:B], ACT.Gelu, bias=mlp_b_sb[:, 2 * l:2 * l + 1]).then_inc(hid0_set, 1)
            for l in range(2):
                act.wait_ge(hid1_mm, l + 1)
                nc.scalar.activation(hidden1[:, l, :], ps[:, 4 + l, 0:B], ACT.Gelu,
                                     bias=mlp_b_sb[:, 2 * l + 1:2 * l + 2]).then_inc(hid1_set, 1)
            for l in range(2):
                act.wait_ge(logits_set, l + 1)
                nc.scalar.activation(expo[:, l, :], logits[:, l, :], ACT.Exp, bias=neg_max[:, l:l + 1],
                                     accum_out=total[:, l:l + 1]).then_inc(expo_set, 1)
            for l in range(2):
                act.wait_ge(mix_in, 16 * (l + 1))
                if l:
                    act.wait_ge(mix_set, l)
                nc.scalar.copy(mix_high, mix_raw).then_inc(mix_high_set, 1)
                act.wait_ge(conv_ident_set, l + 1)
                nc.scalar.copy(conv_parts[2 * l + 1][:, HIGH].rearrange("p g o m -> p (g o m)"), conv_raw[:]).then_inc(conv_high_set, 1)
                for n in range(l * Q, (l + 1) * Q):
                    if n >= Q:
                        act.wait_ge(stored[n % Q], 16)
                    for m in range(0, QB, 2):
                        act.wait_ge(agg_mm, n * QB + m + 1)
                        nc.scalar.copy(stage[n % Q][:, m * N:(m + 1) * N], ps[:, m, :]).then_inc(agg_act, 1)


            def wait_moved(layer, j):
                for g in range(G):
                    act.wait_ge(ph_moved[layer][g], 16 * PH * (j + 1))

            def evacuate(layer, j, s):
                if s == 0:
                    act.wait_ge(bias_set[layer], j + 1)
                for p in range(PH):
                    act.wait_ge(mm[layer], nth(j, s, p))
                    nc.scalar.activation(chan_out[:, p, s, :], ps[:, p, :], ACT.Identity,
                                         bias=bias_col(layer, s, 0)).then_inc(evac[layer], 1)

            def back(layer, j, s, g, dst):
                act.wait_ge(mm[layer], nth(j, s, g))
                for p in range(PH):
                    last = nc.scalar.activation(dst[CG * g:CG * (g + 1), p, :], ps[CG * p:CG * (p + 1), 4 + g, :],
                                                ACT.Identity, bias=bias_col(layer, s, g, CG * p, CG * (p + 1)))
                last.then_inc(back_act[layer], 1)

            def conv_high(layer, j, s, g, user):
                act.wait_ge(ph_moved[layer][g], 16 * PH * (j + 1))
                if user is not None:
                    act.wait_ge(mm[user[0]], nth(user[1], s, g))
                nc.scalar.copy(cv[:, s, HIGH, g, 1:N + 1], ph_in[layer][:, g, s, :]).then_inc(high_set[layer][s], 1)

            def matrix_high(layer, j):
                act.wait_ge(m_in[layer], 16 * (j + 1))
                nc.scalar.copy(m_parts[layer][:, HIGH], m_raw[layer][:]).then_inc(m_high_set[layer], 1)

            def step(i, inner):
                out_v = out_t[:].rearrange("c s (n p) -> c s p n", p=PH)
                now, last, before = has(i, inner, 0), has(i, inner, 1), has(i, inner, 2)

                def evac0(s):
                    if now:
                        if s == 0:
                            if before:
                                wait_moved(3, i - 2)
                            elif i == 1:
                                wait_moved(1, 0)
                            else:
                                act.wait_ge(stored[0], 32)
                        evacuate(0, i, s)

                def evac2(s):
                    if last:
                        if s == 0:
                            if now:
                                wait_moved(1, i)
                            else:
                                wait_moved(3, i - 2)
                        evacuate(2, i - 1, s)

                def back3(s, g):
                    if before:
                        if g == BACK_ACT[3][0]:
                            if s == 0:
                                act.wait_ge(bias_set[3], i - 1)
                            if inner or i > 2:
                                act.wait_ge(out_done[s], 16 * (i - 2))
                        back(3, i - 2, s, g, out_v[:, s])

                def back1(s, g):
                    if now:
                        if s == 0 and g == BACK_ACT[1][0]:
                            act.wait_ge(bias_set[1], i + 1)
                        back(1, i, s, g, chan[:, s])

                def chan_high(s, phases):
                    if last:
                        if phases[0] == 0:
                            act.wait_ge(back_act[1], nth(i - 1, s, BACK_ACT[1][-1], BACK_ACT[1]))
                            act.wait_ge(back_dve[1], nth(i - 1, s, BACK_DVE[1][-1], BACK_DVE[1]))
                            if now:
                                act.wait_ge(mm[0], nth(i, s, PH - 1))
                            elif before:
                                act.wait_ge(mm[2], nth(i - 2, s, PH - 1))
                        for p in phases:
                            nc.scalar.copy(pw[:, s, HIGH, p, :], chan[:, s, p, :]).then_inc(high_set[2][s], 1)

                def high1(s, g):
                    if now:
                        conv_high(1, i, s, g, (3, i - 2) if before else (1, i - 1) if i else None)

                def high3(s, g, lag=2):
                    if has(i, inner, lag):
                        j = i - lag
                        conv_high(3, j, s, g, (1, j + 1) if inner or j + 1 < PAIRS else (3, j - 1))

                high3(0, 1)
                chan_high(0, (0, 1))
                high3(0, 2)
                chan_high(0, (2, 3))
                high3(0, 3)
                evac0(0)
                high3(1, 0)
                high3(1, 1)
                back3(0, 0)
                evac0(1)
                high3(1, 2)
                high3(1, 3)
                if last:
                    matrix_high(2, i - 1)
                back3(1, 0)
                chan_high(1, range(PH))
                high1(0, 0)
                high1(1, 0)
                high1(0, 1)
                high1(1, 1)
                if inner or i + 1 < PAIRS:
                    if i >= 0:
                        act.wait_ge(mm[0], nth(i, 1, PH - 1))
                    matrix_high(0, i + 1)
                high1(0, 2)
                high1(1, 2)
                high1(0, 3)
                back1(0, 0)
                high1(1, 3)
                evac2(0)
                back1(0, 2)
                evac2(1)
                back1(1, 0)
                high3(0, 0, lag=1)
                back1(1, 2)

            steps(act, step)

        @block.vector
        def _(dve):
            chained = [0]

            def chain(ins):
                chained[0] += 1
                ins.then_inc(dve_chain, 1)
                dve.wait_ge(dve_chain, chained[0])

            def table(layer, g):
                return bias_table[:, :, layer * G + g]

            dve.wait_ge(small_in, 16 * LOADS)
            conv_raw_v = conv_raw[:].rearrange("p (g o m) -> p g o m", g=G, o=OFF)

            def conv_identity(l):
                dve.wait_ge(conv_in, 16 * (l + 1))
                for g in range(G):
                    last = nc.vector.tensor_tensor(conv_raw_v[:, g, 1, :], conv_raw_v[:, g, 1, :], ident, ALU.add)
                last.then_inc(conv_ident_set, 1)

            for l in range(2):
                dve.wait_ge(ctx_mm, l + 1)
                for g in range(G):
                    last = nc.vector.tensor_scalar(table(2 * l + 1, g), ps[:, 2 + l, g * B:(g + 1) * B], side_sb[:, g:g + 1], None, ALU.add)
                last.then_inc(ctx_read, 1)
            for l in range(2):
                dve.wait_ge(logit_mm, l + 1)
                chain(nc.vector.tensor_tensor(logits[:, l, :], ps[:, 6 + l, 0:K], b2_sb[:, l, :], ALU.add))
                chain(nc.vector.reduce_max(top[:, l:l + 1], logits[:, l, :], AX_X))
                nc.vector.tensor_scalar(neg_max[:, l:l + 1], top[:, l:l + 1], -1.0, None, ALU.mult).then_inc(logits_set, 1)
            for l in range(2):
                dve.wait_ge(expo_set, l + 1)
                chain(nc.vector.reciprocal(inv[:, l:l + 1], total[:, l:l + 1]))
                chain(nc.vector.tensor_scalar(att_rep[:, l, 0:K], expo[:, l, :], inv[:, l:l + 1], None, ALU.mult))
                width = K
                while width < 128:
                    ins = nc.vector.tensor_copy(att_rep[:, l, width:2 * width], att_rep[:, l, 0:width])
                    width *= 2
                    if width < 128:
                        chain(ins)
                ins.then_inc(att_set, 1)
            for l in range(2):
                dve.wait_ge(att_t_mm, l + 1)
                nc.vector.tensor_copy(att_t[:, l, :], ps[:, l, 0:B]).then_inc(att_t_set, 1)
            dve.wait_ge(att_t_set, 2)
            chain(nc.vector.tensor_copy(att_high, att_t))
            chain(nc.vector.scalar_tensor_tensor(out=att_parts, in0=att_high.bitcast(fp32), scalar=a_low, in1=att_t,
                                                 op0=ALU.mult, op1=ALU.add))
            for q in range(Q):
                last = nc.vector.tensor_scalar(att_q[:, :, q, :], att_parts.bitcast(fp32), in_quarter[:, q:q + 1], None, ALU.mult)
            last.then_inc(att_q_set, 1)
            for l in range(2):
                dve.wait_ge(mix_b_mm, l + 1)
                for g in range(G):
                    last = nc.vector.tensor_copy(table(2 * l, g), ps[:, 4 + l, 0:B])
                last.then_inc(mix_b_read, 1)

            for l in range(2):
                dve.wait_ge(mix_high_set, l + 1)
                if l:
                    dve.wait_ge(agg_mm, Q * QB)
                nc.vector.scalar_tensor_tensor(out=mix_parts, in0=mix_high.bitcast(fp32), scalar=w_low, in1=mix_raw,
                                               op0=ALU.mult, op1=ALU.add).then_inc(mix_set, 1)
                conv_identity(l)
                dve.wait_ge(conv_high_set, l + 1)
                parts = conv_parts[2 * l + 1]
                nc.vector.tensor_tensor(parts[:, LOW].rearrange("p g o m -> p (g o m)"), conv_raw[:],
                                        parts[:, HIGH].bitcast(fp32).rearrange("p g o m -> p (g o m)"),
                                        ALU.subtract).then_inc(conv_set, 1)
                for n in range(l * Q, (l + 1) * Q):
                    if n >= Q:
                        dve.wait_ge(stored[n % Q], 16)
                    for m in range(1, QB, 2):
                        dve.wait_ge(agg_mm, n * QB + m + 1)
                        nc.vector.tensor_copy(stage[n % Q][:, m * N:(m + 1) * N], ps[:, m, :]).then_inc(agg_dve, 1)
                    dve.wait_ge(agg_act, (n + 1) * (QB // 2))
                    dve.wait_ge(agg_dve, (n + 1) * (QB // 2))
                    first = n % Q * (C // Q)
                    diagonal = stage[n % Q][:, first:first + (C + 1) * (C // Q - 1) + 1:C + 1]
                    nc.vector.tensor_scalar(diagonal, diagonal, 1.0, None, ALU.add).then_inc(agg_set, 1)

            dve.wait_ge(agg_mm, 2 * Q * QB)
            for s in range(2):
                last = nc.vector.memset(cv[:, s, :, :, 0:HALO:HALO - 1].bitcast(fp32), 0.0)
            last.then_inc(zeros_set, 1)

            def back(layer, j, s, g, dst):
                dve.wait_ge(mm[layer], nth(j, s, g))
                for p in range(PH):
                    last = nc.vector.tensor_scalar(dst[CG * g:CG * (g + 1), p, :], ps[CG * p:CG * (p + 1), 4 + g, :],
                                                   bias_col(layer, s, g, CG * p, CG * (p + 1)), None, ALU.add)
                last.then_inc(back_dve[layer], 1)

            def conv_low(layer, j, s, g):
                dve.wait_ge(high_set[layer][s], 4 * j + g + 1)
                nc.vector.tensor_tensor(cv[:, s, LOW, g, 1:N + 1], ph_in[layer][:, g, s, :],
                                        cv[:, s, HIGH, g, 1:N + 1].bitcast(fp32), ALU.subtract).then_inc(low_dve[layer], 1)

            def x_high(j, s, last_mm):
                dve.wait_ge(x_in[s], 16 * (j + 1))
                if last_mm is not None:
                    dve.wait_ge(mm[last_mm[0]], nth(last_mm[1], s, PH - 1))
                xv = x_t[:].rearrange("c s (n p) -> c s p n", p=PH)
                for p in range(PH):
                    nc.vector.tensor_copy(pw[:, s, HIGH, p, :], xv[:, s, p, :]).then_inc(high_set[0][s], 1)

            def step(i, inner):
                out_v = out_t[:].rearrange("c s (n p) -> c s p n", p=PH)
                now, last, before = has(i, inner, 0), has(i, inner, 1), has(i, inner, 2)

                def back3(s, g):
                    if before:
                        if g == BACK_DVE[3][0]:
                            if s == 0:
                                dve.wait_ge(bias_set[3], i - 1)
                            if inner or i > 2:
                                dve.wait_ge(out_done[s], 16 * (i - 2))
                        back(3, i - 2, s, g, out_v[:, s])

                def back1(s, g):
                    if now:
                        if s == 0 and g == BACK_DVE[1][0]:
                            dve.wait_ge(bias_set[1], i + 1)
                        back(1, i, s, g, chan[:, s])

                def low1(s, g):
                    if now:
                        conv_low(1, i, s, g)

                def low3(s, g, lag=2):
                    if has(i, inner, lag):
                        conv_low(3, i - lag, s, g)

                def x_parts(s):
                    if inner or i + 1 < PAIRS:
                        x_high(i + 1, s, (2, i - 1) if last else (0, i) if i >= 0 else None)

                low3(0, 1)
                low3(0, 2)
                back3(0, 1)
                low3(1, 0)
                back3(0, 2)
                low3(1, 1)
                low3(1, 2)
                back3(0, 3)
                back3(1, 1)
                back3(1, 2)
                low1(0, 1)
                low1(0, 2)
                back3(1, 3)
                low1(0, 3)
                low1(1, 1)
                low1(1, 2)
                low1(1, 3)
                back1(0, 1)
                x_parts(0)
                back1(0, 3)
                x_parts(1)
                back1(1, 1)
                low3(0, 0, lag=1)
                back1(1, 3)

            steps(dve, step)

        @block.gpsimd
        def _(pool):
            pool.wait_ge(mix_b_read, 2)

            def set_bias(layer, j, first):
                if not first:
                    if layer % 2:
                        pool.wait_ge(back_act[layer], nth(j - 1, 1, BACK_ACT[layer][-1], BACK_ACT[layer]))
                        pool.wait_ge(back_dve[layer], nth(j - 1, 1, BACK_DVE[layer][-1], BACK_DVE[layer]))
                    else:
                        pool.wait_ge(evac[layer], nth(j - 1, 1, PH - 1))
                nc.gpsimd.tensor_copy(bias[layer][:], bias_table[:, bass.ds(2 * j, 2), layer * G:(layer + 1) * G]).then_inc(bias_set[layer], 1)

            def matrix_low(layer, j):
                pool.wait_ge(m_high_set[layer], j + 1)
                nc.gpsimd.tensor_tensor(m_parts[layer][:, LOW], m_raw[layer][:], m_parts[layer][:, HIGH].bitcast(fp32),
                                        ALU.subtract).then_inc(m_set[layer], 1)

            def pointwise_low(layer, j, s, src, phases=range(PH)):
                for p in phases:
                    pool.wait_ge(high_set[layer][s], 4 * j + p + 1)
                    nc.gpsimd.tensor_tensor(pw[:, s, LOW, p, :], src[:, p, :], pw[:, s, HIGH, p, :].bitcast(fp32),
                                            ALU.subtract).then_inc(low_pool[layer], 1)

            def conv_low(layer, j, s):
                for g in LOW_POOL[layer]:
                    pool.wait_ge(high_set[layer][s], 4 * j + g + 1)
                    nc.gpsimd.tensor_tensor(cv[:, s, LOW, g, 1:N + 1], ph_in[layer][:, g, s, :],
                                            cv[:, s, HIGH, g, 1:N + 1].bitcast(fp32), ALU.subtract).then_inc(low_pool[layer], 1)

            def step(i, inner):
                xv = x_t[:].rearrange("c s (n p) -> c s p n", p=PH)
                now, last, before = has(i, inner, 0), has(i, inner, 1), has(i, inner, 2)
                if before:
                    conv_low(3, i - 2, 0)
                if last:
                    set_bias(2, i - 1, not inner and i == 1)
                    pointwise_low(2, i - 1, 0, chan[:, 0])
                if before:
                    conv_low(3, i - 2, 1)
                if now:
                    set_bias(1, i, not inner and i == 0)
                if last:
                    matrix_low(2, i - 1)
                    pointwise_low(2, i - 1, 1, chan[:, 1], (0, 1))
                if now:
                    conv_low(1, i, 0)
                if last:
                    pointwise_low(2, i - 1, 1, chan[:, 1], (2, 3))
                if now:
                    conv_low(1, i, 1)
                if inner or i + 1 < PAIRS:
                    matrix_low(0, i + 1)
                if last:
                    set_bias(3, i - 1, not inner and i == 1)
                if inner or i + 1 < PAIRS:
                    pointwise_low(0, i + 1, 0, xv[:, 0])
                    set_bias(0, i + 1, i < 0 if not inner else False)
                    pointwise_low(0, i + 1, 1, xv[:, 1])

            steps(pool, step)


def kernel(x, cond_128, fside_S_0, **weights):
    import numpy as np
    import concourse.bacc as bacc
    from concourse.bass_utils import run_bass_kernel_spmd

    dense, conv = ("L0_cond_", "L2_cond_"), ("L1_cond_", "L3_cond_")
    w = {name: np.asarray(a) for name, a in weights.items()}
    x, cond, side = np.asarray(x), np.asarray(cond_128), np.asarray(fside_S_0)
    B, C, T = x.shape
    K = w["L0_cond_bias_k"].shape[0]
    G, PH, OFF, Q = 4, 4, 3, 4
    CG = C // G
    TAPS = w["L1_cond_weight"].shape[2]
    HALF = TAPS // 2

    def by_phases(a):
        a = a.reshape(*a.shape[:-1], G, 1, CG)
        return np.broadcast_to(a, (*a.shape[:-2], PH, CG)).reshape(*a.shape[:-2], PH * CG)

    def toeplitz(taps):
        t = np.zeros((PH, CG, G, OFF, PH, CG), taps.dtype)
        v = taps.reshape(G, CG, CG, TAPS)
        for p_in in range(PH):
            for o in range(OFF):
                for p_out in range(PH):
                    tap = PH * (o - 1) + p_in - p_out + HALF
                    if 0 <= tap < TAPS:
                        t[p_in, :, :, o, p_out, :] = v[:, :, :, tap].transpose(2, 0, 1)
        return t.reshape(PH * CG, G * OFF * PH * CG)

    part = np.arange(128)
    copy = part % 32 // K
    consts = np.zeros((128, 134), np.float32)
    consts[:, 0:128] = np.eye(128)
    consts[:, 128] = np.where(copy >= 2, -1, 0)
    consts[:, 129] = -(copy % 2)
    consts[:, 130:134] = part[:, None] // 32 == np.arange(Q)

    def mixing(a):
        a = a[..., 0].transpose(0, 2, 1).reshape(K, Q, 1, C * C // Q).transpose(1, 2, 0, 3)
        return np.broadcast_to(a, (Q, 32 // K, K, C * C // Q)).reshape(128, C * C // Q)

    arrays = {
        "x": x,
        "emb_t": cond.T,
        "mlp_w": np.stack([w[p + n] for p in dense for n in ("W0", "W1")], axis=1),
        "mlp_b": np.stack([w[p + n] for p in dense for n in ("b0", "b1")], axis=1),
        "w2_in": np.stack([w[p + "W2"] for p in dense], axis=1),
        "b2_in": np.broadcast_to(np.stack([w[p + "b2"] for p in dense]), (128, 2, K)),
        "mix_w": np.stack([mixing(w[p + "weight"]) for p in dense]),
        "mix_b": np.stack([w[p + "bias_k"] for p in dense], axis=1),
        "conv_w": np.stack([toeplitz(w[p + "weight"]) for p in conv]),
        "ctx_w": np.stack([by_phases(w[p + "c_weight"].T) for p in conv], axis=1),
        "side": by_phases(side).T,
        "consts": consts,
    }
    arrays = {name: np.ascontiguousarray(a) for name, a in arrays.items()}
    nc = bacc.Bacc("TRN2", target_bir_lowering=False, num_devices=1)
    aps = {name: nc.dram_tensor(name, a.shape, mybir.dt.from_np(a.dtype), kind="ExternalInput").ap()
           for name, a in arrays.items()}
    scratch = nc.dram_tensor("mixed", (2, B, C * C), mybir.dt.float32, kind="Internal").ap()
    out = nc.dram_tensor("out", (B, C, T), mybir.dt.float32, kind="ExternalOutput").ap()
    build_cond_resid(nc, scratch=scratch, out=out, **aps)
    r = run_bass_kernel_spmd(nc, [arrays], core_ids=[0])
    return r.results[0]["out"]
```

```python
import concourse.bass as bass
from concourse import mybir
from contextlib import ExitStack


def build_cond_resid(nc, x, small, mix_w, mix_b, conv_w, consts, scratch, out):
    fp32 = mybir.dt.float32
    f32r = mybir.dt.float32r
    ALU = mybir.AluOpType
    ACT = mybir.ActivationFunctionType
    AX_X = mybir.AxisListType.X

    B, C, T = x.shape
    PAIRS = B // 2
    PH = 4
    G = 4
    CG = C // G
    N = T // PH
    OFF = 3
    K = mix_b.shape[0]
    SMALL = small.shape[1]
    NL = 4
    Q = 4
    QW = C * C // Q
    QB = QW // N
    HALO = N + 2
    HIGH, LOW = 0, 1
    LOADS = 3
    CHUNKS = 4

    ctx = ExitStack()
    with ctx:
        def sb(name, shape, dt=fp32):
            return ctx.enter_context(nc.sbuf_tensor(name, shape, dt))

        def sem(name):
            return ctx.enter_context(nc.semaphore(name))

        x_t = sb("x_t", [128, 2, T])
        pw = sb("pw", [128, 2, 2, PH, N], f32r)
        cv = sb("cv", [128, 2, 2, G, HALO], f32r)
        chan = sb("chan", [128, 2, PH, N])
        chan_out = sb("chan_out", [128, PH, 2, N])
        ph_in = {1: sb("ph_in1", [128, G, 2, N]), 3: sb("ph_in3", [128, G, 2, N])}
        out_t = sb("out_t", [128, 2, T])
        m_raw = {l: sb(f"m_raw{l}", [128, 2, C]) for l in (0, 2)}
        m_parts = {l: sb(f"m_parts{l}", [128, 2, 2, C], f32r) for l in (0, 2)}
        bias = [sb(f"bias{l}", [128, 2, G]) for l in range(NL)]
        conv_parts = {l: sb(f"conv_parts{l}", [128, 2, G, OFF, 128], f32r) for l in (1, 3)}
        bias_table = sb("bias_table", [128, B, NL * G])
        ps = ctx.enter_context(nc.psum_tensor("ps", [128, 8, N], fp32))

        conv_raw = sb("conv_raw", [128, G * OFF * 128])
        consts_sb = sb("consts_sb", [128, 134])
        ident = consts_sb[:, 0:128]
        w_low = consts_sb[:, 128:129]
        a_low = consts_sb[:, 129:130]
        in_quarter = consts_sb[:, 130:134]

        def flat(tile, pattern):
            return tile[:].rearrange(f"lane {pattern} -> lane ({pattern})")

        mix_raw = [flat(out_t, "s t"), flat(ph_in[3], "g s n")]
        mix_high = flat(pw, "s r p n")[:, 0:QW]
        mix_parts = flat(cv, "s r g n")[:, 0:QW]
        room_r = flat(cv, "s r g n")[:, QW:]
        room = flat(chan, "s p n")
        CHAN_OUT, PH_IN1, OUT_T, CHAN, PH_IN3 = range(5)
        stage = [flat(chan_out, "p s n"), flat(ph_in[1], "g s n"), flat(out_t, "s t"), room, flat(ph_in[3], "g s n")]
        SLOT = (CHAN_OUT, PH_IN1, CHAN, OUT_T, CHAN, PH_IN3, OUT_T, PH_IN3)
        taken = {"room": 0, "room_r": 0}

        def part_of(name, shape):
            width = 1
            for n in shape[1:]:
                width *= n
            first = taken[name]
            taken[name] += width
            view = (room if name == "room" else room_r)[0:shape[0], first:first + width]
            names = "abcd"[:len(shape) - 1]
            return view if len(shape) == 2 else view.rearrange(
                f"p ({' '.join(names)}) -> p {' '.join(names)}", **dict(zip(names, shape[1:])))

        emb_sb = part_of("room", [128, B])
        mlp_w_sb = part_of("room", [128, 4, 128])
        ctx_w_sb = part_of("room", [128, 2, G, 128])
        mlp_b_sb = part_of("room", [128, 4])
        w2_sb = part_of("room", [128, 2, K])
        b2_sb = part_of("room", [128, 2, K])
        side_sb = part_of("room", [128, G])
        assert taken["room"] == SMALL
        mix_b_sb = part_of("room", [K, 2, 128])
        hidden0 = part_of("room", [128, 2, B])
        hidden1 = part_of("room", [128, 2, B])
        att_rep = part_of("room", [128, 2, 128])
        att_t = part_of("room", [128, 2, B])
        att_high = part_of("room_r", [128, 2, B])
        att_parts = part_of("room_r", [128, 2, B])
        att_q = part_of("room_r", [128, 2, Q, B])
        logits = sb("logits", [128, 2, K])
        expo = sb("expo", [128, 2, K])
        top, neg_max, total, inv = (sb(n, [128, 2]) for n in ("top", "neg_max", "total", "inv"))

        small_in = sem("small_in")
        mix_in = [sem(f"mix_in{l}") for l in range(2)]
        conv_in = sem("conv_in")
        hid0_mm, ctx_mm, hid1_mm = sem("hid0_mm"), sem("ctx_mm"), sem("hid1_mm")
        logit_mm, att_t_mm, mix_b_mm = sem("logit_mm"), sem("att_t_mm"), sem("mix_b_mm")
        agg_mm = sem("agg_mm")
        hid0_set, hid1_set, expo_set = sem("hid0_set"), sem("hid1_set"), sem("expo_set")
        mix_high_set, conv_high_set = sem("mix_high_set"), sem("conv_high_set")
        agg_act = sem("agg_act")
        dve_chain = sem("dve_chain")
        logits_set, ctx_read, att_set = sem("logits_set"), sem("ctx_read"), sem("att_set")
        att_t_set, att_q_set, mix_b_read = sem("att_t_set"), sem("att_q_set"), sem("mix_b_read")
        mix_set, conv_ident_set, conv_set = sem("mix_set"), sem("conv_ident_set"), sem("conv_set")
        agg_dve = sem("agg_dve")
        agg_set = sem("agg_set")
        zeros_set = sem("zeros_set")
        stored = [sem(f"stored{s}") for s in range(len(stage))]

        x_in = [sem(f"x_in{s}") for s in range(2)]
        m_in = {l: sem(f"m_in{l}") for l in (0, 2)}
        ph_moved = {l: [sem(f"ph_moved{l}_{g}") for g in range(G)] for l in (1, 3)}
        out_done = [sem(f"out_done{s}") for s in range(2)]
        mm = [sem(f"mm{l}") for l in range(NL)]
        evac = {l: sem(f"evac{l}") for l in (0, 2)}
        back_act = {l: sem(f"back_act{l}") for l in (1, 3)}
        back_dve = {l: sem(f"back_dve{l}") for l in (1, 3)}
        high_set = [[sem(f"high_set{l}_{s}") for s in range(2)] for l in range(NL)]
        low_dve = {l: sem(f"low_dve{l}") for l in (1, 3)}
        low_pool = [sem(f"low_pool{l}") for l in range(NL)]
        m_high_set = {l: sem(f"m_high_set{l}") for l in (0, 2)}
        m_set = {l: sem(f"m_set{l}") for l in (0, 2)}
        bias_set = [sem(f"bias_set{l}") for l in range(NL)]

        BACK_ACT = {1: (0, 2), 3: (0,)}
        BACK_DVE = {1: (1, 3), 3: (1, 2, 3)}
        LOW_DVE = {1: (1, 2, 3), 3: (0, 1, 2)}
        LOW_POOL = {1: (0,), 3: (3,)}

        def nth(j, s, k, mine=(0, 1, 2, 3)):
            return len(mine) * (2 * j + s) + mine.index(k) + 1

        def steps(engine, step):
            for i in range(3):
                step(i, False)
            with engine.Fori(3, PAIRS - 2) as i:
                step(i, True)
            for i in range(PAIRS - 2, PAIRS + 2):
                step(i, False)

        def has(i, inner, lag):
            return inner or 0 <= i - lag < PAIRS

        def bias_col(layer, s, g, p0=0, p1=128):
            return bias[layer][p0:p1, s, g:g + 1]

        def uses(n):
            return SLOT[:n].count(SLOT[n])

        block = ctx.enter_context(nc.Block())

        @block.sync
        def _(sp):
            sp.dma_start(room[:, 0:SMALL], small).then_inc(small_in, 16)
            sp.dma_start(consts_sb[:], consts).then_inc(small_in, 16)
            sp.dma_start(mix_b_sb, mix_b).then_inc(small_in, 16)
            sp.dma_start(mix_raw[0], mix_w[0]).then_inc(mix_in[0], 16)
            sp.dma_start(conv_raw[:], conv_w[0]).then_inc(conv_in, 16)
            sp.dma_start(mix_raw[1], mix_w[1]).then_inc(mix_in[1], 16)

            def store_quarter(n):
                sp.wait_ge(agg_set, n + 1)
                sp.dma_start(scratch[n // Q][:, n % Q * QW:(n % Q + 1) * QW], stage[SLOT[n]]).then_inc(stored[SLOT[n]], 16)

            def load_matrices(l, j):
                sp.dma_start(m_raw[l][:], scratch[l // 2][bass.ds(2 * j, 2)].rearrange("s (i o) -> i s o", i=C)).then_inc(m_in[l], 16)

            def load_x(j, s):
                sp.dma_start(x_t[:, s, :], x[2 * j + s]).then_inc(x_in[s], 16)

            for s in range(2):
                load_x(0, s)
            for n in range(Q):
                store_quarter(n)
            for n in range(Q):
                sp.wait_ge(stored[SLOT[n]], 16 * (uses(n) + 1))
            load_matrices(0, 0)
            for n in (Q, Q + 1):
                store_quarter(n)

            def to_phases(layer, j):
                for g in range(G):
                    for p in range(PH):
                        if g == 0:
                            sp.wait_ge(evac[layer - 1], nth(j, 1, p))
                        sp.dma_start(ph_in[layer][CG * p:CG * (p + 1), g], chan_out[CG * g:CG * (g + 1), p]).then_inc(ph_moved[layer][g], 16)

            def wait_parts(layer, j):
                sp.wait_ge(low_pool[layer], nth(j, 1, LOW_POOL[layer][-1], LOW_POOL[layer]))
                sp.wait_ge(low_dve[layer], nth(j, 1, LOW_DVE[layer][-1], LOW_DVE[layer]))

            def store_out(j, s):
                sp.wait_ge(back_act[3], nth(j, s, BACK_ACT[3][-1], BACK_ACT[3]))
                sp.wait_ge(back_dve[3], nth(j, s, BACK_DVE[3][-1], BACK_DVE[3]))
                sp.dma_start(out[2 * j + s], out_t[:, s, :]).then_inc(out_done[s], 16)

            def step(i, inner):
                if has(i, inner, 0):
                    if inner or i >= 1:
                        wait_parts(1, i - 1)
                    to_phases(1, i)
                if not inner and i == 0:
                    step(-1, False)
                    sp.wait_ge(conv_set, 1)
                    sp.dma_start(conv_raw[:], conv_w[1]).then_inc(conv_in, 16)
                    for n in (Q + 2, Q + 3):
                        store_quarter(n)
                    for n in range(Q, 2 * Q):
                        sp.wait_ge(stored[SLOT[n]], 16 * (uses(n) + 1))
                    load_matrices(2, 0)
                if has(i, inner, 2):
                    store_out(i - 2, 0)
                    store_out(i - 2, 1)
                if has(i, inner, 1):
                    if has(i, inner, 2):
                        wait_parts(3, i - 2)
                    to_phases(3, i - 1)
                if inner or 1 <= i < PAIRS:
                    sp.wait_ge(m_set[2], i)
                    load_matrices(2, i)
                if inner or -1 <= i < PAIRS - 2:
                    sp.wait_ge(m_set[0], i + 2)
                    load_matrices(0, i + 2)
                    for s in range(2):
                        sp.wait_ge(low_pool[0], nth(i + 1, s, PH - 1))
                        load_x(i + 2, s)

            steps(sp, step)
            for s in range(2):
                sp.wait_ge(out_done[s], 16 * PAIRS)

        @block.tensor
        def _(pe):
            pe.wait_ge(small_in, 16 * LOADS)
            for l in range(2):
                nc.tensor.matmul(ps[:, l, 0:B], mlp_w_sb[:, 2 * l, :], emb_sb, start=True, stop=True).then_inc(hid0_mm, 1)
            for l in range(2):
                for g in range(G):
                    last = nc.tensor.matmul(ps[:, 2 + l, g * B:(g + 1) * B], ctx_w_sb[:, l, g, :], emb_sb, start=True, stop=True)
                last.then_inc(ctx_mm, 1)
            for l in range(2):
                pe.wait_ge(hid0_set, l + 1)
                nc.tensor.matmul(ps[:, 4 + l, 0:B], mlp_w_sb[:, 2 * l + 1, :], hidden0[:, l, :], start=True, stop=True).then_inc(hid1_mm, 1)
            for l in range(2):
                pe.wait_ge(hid1_set, l + 1)
                nc.tensor.matmul(ps[:, 6 + l, 0:K], hidden1[:, l, :], w2_sb[:, l, :], start=True, stop=True).then_inc(logit_mm, 1)
            for l in range(2):
                pe.wait_ge(att_set, l + 1)
                nc.tensor.matmul(ps[:, l, 0:B], att_rep[:, l, :], ident, start=True, stop=True).then_inc(att_t_mm, 1)
            for l in range(2):
                pe.wait_ge(att_t_set, l + 1)
                nc.tensor.matmul(ps[:, 4 + l, 0:B], mix_b_sb[:, l, :], att_t[0:K, l, :], start=True, stop=True).then_inc(mix_b_mm, 1)
            pe.wait_ge(att_q_set, 1)
            pe.wait_ge(ctx_read, 2)
            pe.wait_ge(mix_b_read, 2)

            def mixed_out(n):
                return lambda m: pe.wait_ge((agg_act, agg_dve)[m % 2], n * (QB // 2) + m // 2 + 1)

            def mix_quarter(n, wait_bank):
                for m in range(QB):
                    if m % (QB // CHUNKS) == 0:
                        pe.wait_ge(mix_set, n // Q * CHUNKS + m // (QB // CHUNKS) + 1)
                    wait_bank(m)
                    nc.tensor.matmul(ps[:, m, :], att_q[:, n // Q, n % Q, :], mix_parts[:, m * N:(m + 1) * N],
                                     start=True, stop=True).then_inc(agg_mm, 1)

            def free(k):
                pass

            for n in range(2 * Q - 1):
                mix_quarter(n, mixed_out(n - 1) if n else free)

            def pointwise(layer, j, s, wait_bank):
                for p in range(PH):
                    pe.wait_ge(low_pool[layer], nth(j, s, p))
                    wait_bank(p)
                    for n, (m, a) in enumerate(((HIGH, HIGH), (HIGH, LOW), (LOW, HIGH))):
                        last = nc.tensor.matmul(ps[:, p, :], m_parts[layer][:, m, s, :], pw[:, s, a, p, :],
                                                start=(n == 0), stop=(n == 2))
                    last.then_inc(mm[layer], 1)

            def convolution(layer, j, s, wait_bank):
                passes = [(w, a, o) for o in range(OFF) for w, a in ((HIGH, HIGH), (HIGH, LOW), (LOW, HIGH))]
                for g in range(G):
                    if g in LOW_DVE[layer]:
                        pe.wait_ge(low_dve[layer], nth(j, s, g, LOW_DVE[layer]))
                    else:
                        pe.wait_ge(low_pool[layer], nth(j, s, g, LOW_POOL[layer]))
                    wait_bank(g)
                    for n, (w, a, o) in enumerate(passes):
                        last = nc.tensor.matmul(ps[:, 4 + g, :], conv_parts[layer][:, w, g, o, :], cv[:, s, a, g, o:o + N],
                                                start=(n == 0), stop=(n == len(passes) - 1))
                    last.then_inc(mm[layer], 1)

            def evacuated(layer, j, s):
                return lambda p: pe.wait_ge(evac[layer], nth(j, s, p))

            def taken_back(layer, j, s):
                def wait(g):
                    if g in BACK_ACT[layer]:
                        pe.wait_ge(back_act[layer], nth(j, s, g, BACK_ACT[layer]))
                    else:
                        pe.wait_ge(back_dve[layer], nth(j, s, g, BACK_DVE[layer]))
                return wait

            def step(i, inner):
                now, last, before = has(i, inner, 0), has(i, inner, 1), has(i, inner, 2)
                if now:
                    pe.wait_ge(m_set[0], i + 1)
                    pointwise(0, i, 0, evacuated(2, i - 2, 1) if before else evacuated(0, i - 1, 1) if i else mixed_out(2 * Q - 2))
                if not inner and i == 2:
                    pe.wait_ge(conv_set, 2)
                if before:
                    convolution(3, i - 2, 0, taken_back(1, i - 1, 1) if last else taken_back(3, i - 3, 1))
                if now:
                    pointwise(0, i, 1, evacuated(0, i, 0))
                if not inner and i == 0:
                    evacuated_0, copied = evacuated(0, 0, 1), mixed_out(2 * Q - 2)
                    mix_quarter(2 * Q - 1, lambda m: (evacuated_0 if m < PH else copied)(m))
                    pe.wait_ge(conv_set, 1)
                    pe.wait_ge(zeros_set, 1)
                    for m in range(QB):
                        mixed_out(2 * Q - 1)(m)
                if before:
                    convolution(3, i - 2, 1, taken_back(3, i - 2, 0))
                if last:
                    pe.wait_ge(m_set[2], i)
                    pointwise(2, i - 1, 0, evacuated(0, i, 1) if now else evacuated(2, i - 2, 1))
                if now:
                    convolution(1, i, 0, taken_back(3, i - 2, 1) if before else taken_back(1, i - 1, 1) if i else free)
                if last:
                    pointwise(2, i - 1, 1, evacuated(2, i - 1, 0))
                if now:
                    convolution(1, i, 1, taken_back(1, i, 0))

            steps(pe, step)

        @block.scalar
        def _(act):
            act.wait_ge(small_in, 16 * LOADS)
            for l in range(2):
                act.wait_ge(hid0_mm, l + 1)
                nc.scalar.activation(hidden0[:, l, :], ps[:, l, 0:B], ACT.Gelu, bias=mlp_b_sb[:, 2 * l:2 * l + 1]).then_inc(hid0_set, 1)
            for l in range(2):
                act.wait_ge(hid1_mm, l + 1)
                nc.scalar.activation(hidden1[:, l, :], ps[:, 4 + l, 0:B], ACT.Gelu,
                                     bias=mlp_b_sb[:, 2 * l + 1:2 * l + 2]).then_inc(hid1_set, 1)
            for l in range(2):
                act.wait_ge(logits_set, l + 1)
                nc.scalar.activation(expo[:, l, :], logits[:, l, :], ACT.Exp, bias=neg_max[:, l:l + 1],
                                     accum_out=total[:, l:l + 1]).then_inc(expo_set, 1)

            def table(layer, g):
                return bias_table[:, :, layer * G + g]

            def mix_high_part(l):
                act.wait_ge(mix_in[l], 16)
                if l:
                    act.wait_ge(mix_set, CHUNKS)
                nc.scalar.copy(mix_high, mix_raw[l]).then_inc(mix_high_set, 1)

            def conv_high_part(l):
                act.wait_ge(conv_ident_set, l + 1)
                nc.scalar.copy(conv_parts[2 * l + 1][:, HIGH].rearrange("p g o m -> p (g o m)"), conv_raw[:]).then_inc(conv_high_set, 1)

            def copy_quarter(n):
                if uses(n):
                    act.wait_ge(stored[SLOT[n]], 16 * uses(n))
                for m in range(0, QB, 2):
                    act.wait_ge(agg_mm, n * QB + m + 1)
                    nc.scalar.copy(stage[SLOT[n]][:, m * N:(m + 1) * N], ps[:, m, :]).then_inc(agg_act, 1)

            mix_high_part(0)
            for l in range(2):
                act.wait_ge(mix_b_mm, l + 1)
                for g in range(G):
                    last = nc.scalar.copy(table(2 * l, g), ps[:, 4 + l, 0:B])
                last.then_inc(mix_b_read, 1)
            copy_quarter(0)
            conv_high_part(0)
            copy_quarter(1)
            mix_high_part(1)
            copy_quarter(2)
            copy_quarter(3)
            copy_quarter(4)
            copy_quarter(5)
            copy_quarter(6)

            def wait_moved(layer, j):
                for g in range(G):
                    act.wait_ge(ph_moved[layer][g], 16 * PH * (j + 1))

            def evacuate(layer, j, s):
                if s == 0:
                    act.wait_ge(bias_set[layer], j + 1)
                for p in range(PH):
                    act.wait_ge(mm[layer], nth(j, s, p))
                    nc.scalar.activation(chan_out[:, p, s, :], ps[:, p, :], ACT.Identity,
                                         bias=bias_col(layer, s, 0)).then_inc(evac[layer], 1)

            def back(layer, j, s, g, dst):
                act.wait_ge(mm[layer], nth(j, s, g))
                for p in range(PH):
                    last = nc.scalar.activation(dst[CG * g:CG * (g + 1), p, :], ps[CG * p:CG * (p + 1), 4 + g, :],
                                                ACT.Identity, bias=bias_col(layer, s, g, CG * p, CG * (p + 1)))
                last.then_inc(back_act[layer], 1)

            def conv_high(layer, j, s, g, user):
                act.wait_ge(ph_moved[layer][g], 16 * PH * (j + 1))
                if user is not None:
                    act.wait_ge(mm[user[0]], nth(user[1], s, g))
                nc.scalar.copy(cv[:, s, HIGH, g, 1:N + 1], ph_in[layer][:, g, s, :]).then_inc(high_set[layer][s], 1)

            def matrix_high(layer, j):
                act.wait_ge(m_in[layer], 16 * (j + 1))
                nc.scalar.copy(m_parts[layer][:, HIGH], m_raw[layer][:]).then_inc(m_high_set[layer], 1)

            def step(i, inner):
                out_v = out_t[:].rearrange("c s (n p) -> c s p n", p=PH)
                now, last, before = has(i, inner, 0), has(i, inner, 1), has(i, inner, 2)

                def evac0(s):
                    if now:
                        if s == 0:
                            if before:
                                wait_moved(3, i - 2)
                            elif i == 1:
                                wait_moved(1, 0)
                            else:
                                act.wait_ge(stored[CHAN_OUT], 16)
                        evacuate(0, i, s)

                def evac2(s):
                    if last:
                        if s == 0:
                            if now:
                                wait_moved(1, i)
                            else:
                                wait_moved(3, i - 2)
                        evacuate(2, i - 1, s)

                def back3(s, g):
                    if before:
                        if g == BACK_ACT[3][0]:
                            if s == 0:
                                act.wait_ge(bias_set[3], i - 1)
                                if not inner and i == 2:
                                    act.wait_ge(stored[OUT_T], 32)
                            if inner or i > 2:
                                act.wait_ge(out_done[s], 16 * (i - 2))
                        back(3, i - 2, s, g, out_v[:, s])

                def back1(s, g):
                    if now:
                        if s == 0 and g == BACK_ACT[1][0]:
                            act.wait_ge(bias_set[1], i + 1)
                            if not inner and i == 0:
                                act.wait_ge(stored[CHAN], 32)
                        back(1, i, s, g, chan[:, s])

                def chan_high(s, phases):
                    if last:
                        if phases[0] == 0:
                            act.wait_ge(back_act[1], nth(i - 1, s, BACK_ACT[1][-1], BACK_ACT[1]))
                            act.wait_ge(back_dve[1], nth(i - 1, s, BACK_DVE[1][-1], BACK_DVE[1]))
                            if now:
                                act.wait_ge(mm[0], nth(i, s, PH - 1))
                            elif before:
                                act.wait_ge(mm[2], nth(i - 2, s, PH - 1))
                        for p in phases:
                            nc.scalar.copy(pw[:, s, HIGH, p, :], chan[:, s, p, :]).then_inc(high_set[2][s], 1)

                def high1(s, g):
                    if now:
                        conv_high(1, i, s, g, (3, i - 2) if before else (1, i - 1) if i else None)

                def high3(s, g, lag=2):
                    if has(i, inner, lag):
                        j = i - lag
                        conv_high(3, j, s, g, (1, j + 1) if inner or j + 1 < PAIRS else (3, j - 1))

                high3(0, 1)
                chan_high(0, (0, 1))
                high3(0, 2)
                chan_high(0, (2, 3))
                high3(0, 3)
                evac0(0)
                high3(1, 0)
                high3(1, 1)
                back3(0, 0)
                evac0(1)
                if not inner and i == 0:
                    copy_quarter(2 * Q - 1)
                    act.wait_ge(agg_mm, 2 * Q * QB)
                if not inner and i == 1:
                    conv_high_part(1)
                high3(1, 2)
                high3(1, 3)
                if last:
                    matrix_high(2, i - 1)
                back3(1, 0)
                chan_high(1, range(PH))
                high1(0, 0)
                high1(1, 0)
                high1(0, 1)
                high1(1, 1)
                if inner or i + 1 < PAIRS:
                    if i >= 0:
                        act.wait_ge(mm[0], nth(i, 1, PH - 1))
                    matrix_high(0, i + 1)
                high1(0, 2)
                high1(1, 2)
                high1(0, 3)
                back1(0, 0)
                high1(1, 3)
                evac2(0)
                back1(0, 2)
                evac2(1)
                back1(1, 0)
                high3(0, 0, lag=1)
                back1(1, 2)

            step(-1, False)
            steps(act, step)

        @block.vector
        def _(dve):
            chained = [0]

            def chain(ins):
                chained[0] += 1
                ins.then_inc(dve_chain, 1)
                dve.wait_ge(dve_chain, chained[0])

            def table(layer, g):
                return bias_table[:, :, layer * G + g]

            dve.wait_ge(small_in, 16 * LOADS)
            conv_raw_v = conv_raw[:].rearrange("p (g o m) -> p g o m", g=G, o=OFF)

            def conv_identity(l):
                dve.wait_ge(conv_in, 16 * (l + 1))
                for g in range(G):
                    last = nc.vector.tensor_tensor(conv_raw_v[:, g, 1, :], conv_raw_v[:, g, 1, :], ident, ALU.add)
                last.then_inc(conv_ident_set, 1)

            for l in range(2):
                dve.wait_ge(ctx_mm, l + 1)
                for g in range(G):
                    last = nc.vector.tensor_scalar(table(2 * l + 1, g), ps[:, 2 + l, g * B:(g + 1) * B], side_sb[:, g:g + 1], None, ALU.add)
                last.then_inc(ctx_read, 1)
            for l in range(2):
                dve.wait_ge(logit_mm, l + 1)
                chain(nc.vector.tensor_tensor(logits[:, l, :], ps[:, 6 + l, 0:K], b2_sb[:, l, :], ALU.add))
                chain(nc.vector.reduce_max(top[:, l:l + 1], logits[:, l, :], AX_X))
                nc.vector.tensor_scalar(neg_max[:, l:l + 1], top[:, l:l + 1], -1.0, None, ALU.mult).then_inc(logits_set, 1)
            for l in range(2):
                dve.wait_ge(expo_set, l + 1)
                chain(nc.vector.reciprocal(inv[:, l:l + 1], total[:, l:l + 1]))
                chain(nc.vector.tensor_scalar(att_rep[:, l, 0:K], expo[:, l, :], inv[:, l:l + 1], None, ALU.mult))
                width = K
                while width < 128:
                    ins = nc.vector.tensor_copy(att_rep[:, l, width:2 * width], att_rep[:, l, 0:width])
                    width *= 2
                    if width < 128:
                        chain(ins)
                ins.then_inc(att_set, 1)
            for l in range(2):
                dve.wait_ge(att_t_mm, l + 1)
                nc.vector.tensor_copy(att_t[:, l, :], ps[:, l, 0:B]).then_inc(att_t_set, 1)
            dve.wait_ge(att_t_set, 2)
            chain(nc.vector.tensor_copy(att_high, att_t))
            chain(nc.vector.scalar_tensor_tensor(out=att_parts, in0=att_high.bitcast(fp32), scalar=a_low, in1=att_t,
                                                 op0=ALU.mult, op1=ALU.add))
            for q in range(Q):
                last = nc.vector.tensor_scalar(att_q[:, :, q, :], att_parts.bitcast(fp32), in_quarter[:, q:q + 1], None, ALU.mult)
            last.then_inc(att_q_set, 1)

            def mixing_parts(l):
                dve.wait_ge(mix_high_set, l + 1)
                for c in range(CHUNKS):
                    if l:
                        dve.wait_ge(agg_mm, (Q - 1) * QB + (c + 1) * (QB // CHUNKS))
                    chunk = slice(c * (QW // CHUNKS), (c + 1) * (QW // CHUNKS))
                    nc.vector.scalar_tensor_tensor(out=mix_parts[:, chunk], in0=mix_high[:, chunk].bitcast(fp32), scalar=w_low,
                                                   in1=mix_raw[l][:, chunk], op0=ALU.mult, op1=ALU.add).then_inc(mix_set, 1)

            def conv_low_part(l):
                dve.wait_ge(conv_high_set, l + 1)
                parts = conv_parts[2 * l + 1]
                nc.vector.tensor_tensor(parts[:, LOW].rearrange("p g o m -> p (g o m)"), conv_raw[:],
                                        parts[:, HIGH].bitcast(fp32).rearrange("p g o m -> p (g o m)"),
                                        ALU.subtract).then_inc(conv_set, 1)

            def copy_quarter(n):
                if uses(n):
                    dve.wait_ge(stored[SLOT[n]], 16 * uses(n))
                for m in range(1, QB, 2):
                    dve.wait_ge(agg_mm, n * QB + m + 1)
                    nc.vector.tensor_copy(stage[SLOT[n]][:, m * N:(m + 1) * N], ps[:, m, :]).then_inc(agg_dve, 1)
                dve.wait_ge(agg_act, (n + 1) * (QB // 2))
                dve.wait_ge(agg_dve, (n + 1) * (QB // 2))
                first = n % Q * (C // Q)
                diagonal = stage[SLOT[n]][:, first:first + (C + 1) * (C // Q - 1) + 1:C + 1]
                nc.vector.tensor_scalar(diagonal, diagonal, 1.0, None, ALU.add).then_inc(agg_set, 1)

            def zeros_beside_phases():
                dve.wait_ge(agg_mm, 2 * Q * QB)
                for s in range(2):
                    last = nc.vector.memset(cv[:, s, :, :, 0:HALO:HALO - 1].bitcast(fp32), 0.0)
                last.then_inc(zeros_set, 1)

            def back(layer, j, s, g, dst):
                dve.wait_ge(mm[layer], nth(j, s, g))
                for p in range(PH):
                    last = nc.vector.tensor_scalar(dst[CG * g:CG * (g + 1), p, :], ps[CG * p:CG * (p + 1), 4 + g, :],
                                                   bias_col(layer, s, g, CG * p, CG * (p + 1)), None, ALU.add)
                last.then_inc(back_dve[layer], 1)

            def conv_low(layer, j, s, g):
                dve.wait_ge(high_set[layer][s], 4 * j + g + 1)
                nc.vector.tensor_tensor(cv[:, s, LOW, g, 1:N + 1], ph_in[layer][:, g, s, :],
                                        cv[:, s, HIGH, g, 1:N + 1].bitcast(fp32), ALU.subtract).then_inc(low_dve[layer], 1)

            def x_high(j, s, last_mm):
                dve.wait_ge(x_in[s], 16 * (j + 1))
                if last_mm is not None:
                    dve.wait_ge(mm[last_mm[0]], nth(last_mm[1], s, PH - 1))
                xv = x_t[:].rearrange("c s (n p) -> c s p n", p=PH)
                for p in range(PH):
                    nc.vector.tensor_copy(pw[:, s, HIGH, p, :], xv[:, s, p, :]).then_inc(high_set[0][s], 1)

            def step(i, inner):
                out_v = out_t[:].rearrange("c s (n p) -> c s p n", p=PH)
                now, last, before = has(i, inner, 0), has(i, inner, 1), has(i, inner, 2)

                def back3(s, g):
                    if before:
                        if g == BACK_DVE[3][0]:
                            if s == 0:
                                dve.wait_ge(bias_set[3], i - 1)
                                if not inner and i == 2:
                                    dve.wait_ge(stored[OUT_T], 32)
                            if inner or i > 2:
                                dve.wait_ge(out_done[s], 16 * (i - 2))
                        back(3, i - 2, s, g, out_v[:, s])

                def back1(s, g):
                    if now:
                        if s == 0 and g == BACK_DVE[1][0]:
                            dve.wait_ge(bias_set[1], i + 1)
                            if not inner and i == 0:
                                dve.wait_ge(stored[CHAN], 32)
                        back(1, i, s, g, chan[:, s])

                def low1(s, g):
                    if now:
                        conv_low(1, i, s, g)

                def low3(s, g, lag=2):
                    if has(i, inner, lag):
                        conv_low(3, i - lag, s, g)

                def x_parts(s):
                    if inner or i + 1 < PAIRS:
                        x_high(i + 1, s, (2, i - 1) if last else (0, i) if i >= 0 else None)

                if not inner and i == 0:
                    copy_quarter(2 * Q - 1)
                    zeros_beside_phases()
                if not inner and i == 1:
                    conv_identity(1)
                    conv_low_part(1)
                low3(0, 1)
                low3(0, 2)
                back3(0, 1)
                low3(1, 0)
                back3(0, 2)
                low3(1, 1)
                low3(1, 2)
                back3(0, 3)
                back3(1, 1)
                back3(1, 2)
                low1(0, 1)
                low1(0, 2)
                back3(1, 3)
                low1(0, 3)
                low1(1, 1)
                low1(1, 2)
                low1(1, 3)
                back1(0, 1)
                x_parts(0)
                back1(0, 3)
                x_parts(1)
                back1(1, 1)
                low3(0, 0, lag=1)
                back1(1, 3)

            mixing_parts(0)
            copy_quarter(0)
            conv_identity(0)
            copy_quarter(1)
            conv_low_part(0)
            copy_quarter(2)
            copy_quarter(3)
            mixing_parts(1)
            dve.wait_ge(mix_set, 2 * CHUNKS)
            step(-1, False)
            copy_quarter(4)
            copy_quarter(5)
            copy_quarter(6)
            steps(dve, step)

        @block.gpsimd
        def _(pool):
            pool.wait_ge(mix_b_read, 2)

            def set_bias(layer, j, first):
                if not first:
                    if layer % 2:
                        pool.wait_ge(back_act[layer], nth(j - 1, 1, BACK_ACT[layer][-1], BACK_ACT[layer]))
                        pool.wait_ge(back_dve[layer], nth(j - 1, 1, BACK_DVE[layer][-1], BACK_DVE[layer]))
                    else:
                        pool.wait_ge(evac[layer], nth(j - 1, 1, PH - 1))
                nc.gpsimd.tensor_copy(bias[layer][:], bias_table[:, bass.ds(2 * j, 2), layer * G:(layer + 1) * G]).then_inc(bias_set[layer], 1)

            def matrix_low(layer, j):
                pool.wait_ge(m_high_set[layer], j + 1)
                nc.gpsimd.tensor_tensor(m_parts[layer][:, LOW], m_raw[layer][:], m_parts[layer][:, HIGH].bitcast(fp32),
                                        ALU.subtract).then_inc(m_set[layer], 1)

            def pointwise_low(layer, j, s, src, phases=range(PH)):
                for p in phases:
                    pool.wait_ge(high_set[layer][s], 4 * j + p + 1)
                    nc.gpsimd.tensor_tensor(pw[:, s, LOW, p, :], src[:, p, :], pw[:, s, HIGH, p, :].bitcast(fp32),
                                            ALU.subtract).then_inc(low_pool[layer], 1)

            def conv_low(layer, j, s):
                for g in LOW_POOL[layer]:
                    pool.wait_ge(high_set[layer][s], 4 * j + g + 1)
                    nc.gpsimd.tensor_tensor(cv[:, s, LOW, g, 1:N + 1], ph_in[layer][:, g, s, :],
                                            cv[:, s, HIGH, g, 1:N + 1].bitcast(fp32), ALU.subtract).then_inc(low_pool[layer], 1)

            def step(i, inner):
                xv = x_t[:].rearrange("c s (n p) -> c s p n", p=PH)
                now, last, before = has(i, inner, 0), has(i, inner, 1), has(i, inner, 2)
                if before:
                    conv_low(3, i - 2, 0)
                if last:
                    set_bias(2, i - 1, not inner and i == 1)
                    pointwise_low(2, i - 1, 0, chan[:, 0])
                if before:
                    conv_low(3, i - 2, 1)
                if now:
                    set_bias(1, i, not inner and i == 0)
                if last:
                    matrix_low(2, i - 1)
                    pointwise_low(2, i - 1, 1, chan[:, 1], (0, 1))
                if now:
                    conv_low(1, i, 0)
                if last:
                    pointwise_low(2, i - 1, 1, chan[:, 1], (2, 3))
                if now:
                    conv_low(1, i, 1)
                if inner or i + 1 < PAIRS:
                    matrix_low(0, i + 1)
                if last:
                    set_bias(3, i - 1, not inner and i == 1)
                if inner or i + 1 < PAIRS:
                    pointwise_low(0, i + 1, 0, xv[:, 0])
                    set_bias(0, i + 1, False)
                    pointwise_low(0, i + 1, 1, xv[:, 1])

            xv = x_t[:].rearrange("c s (n p) -> c s p n", p=PH)
            pointwise_low(0, 0, 0, xv[:, 0])
            matrix_low(0, 0)
            set_bias(0, 0, True)
            pointwise_low(0, 0, 1, xv[:, 1])
            steps(pool, step)


def kernel(x, cond_128, fside_S_0, **weights):
    import numpy as np
    import concourse.bacc as bacc
    from concourse.bass_utils import run_bass_kernel_spmd

    dense, conv = ("L0_cond_", "L2_cond_"), ("L1_cond_", "L3_cond_")
    w = {name: np.asarray(a) for name, a in weights.items()}
    x, cond, side = np.asarray(x), np.asarray(cond_128), np.asarray(fside_S_0)
    B, C, T = x.shape
    K = w["L0_cond_bias_k"].shape[0]
    G, PH, OFF, Q = 4, 4, 3, 4
    CG = C // G
    TAPS = w["L1_cond_weight"].shape[2]
    HALF = TAPS // 2

    def by_phases(a):
        a = a.reshape(*a.shape[:-1], G, 1, CG)
        return np.broadcast_to(a, (*a.shape[:-2], PH, CG)).reshape(*a.shape[:-2], PH * CG)

    def toeplitz(taps):
        t = np.zeros((PH, CG, G, OFF, PH, CG), taps.dtype)
        v = taps.reshape(G, CG, CG, TAPS)
        for p_in in range(PH):
            for o in range(OFF):
                for p_out in range(PH):
                    tap = PH * (o - 1) + p_in - p_out + HALF
                    if 0 <= tap < TAPS:
                        t[p_in, :, :, o, p_out, :] = v[:, :, :, tap].transpose(2, 0, 1)
        return t.reshape(PH * CG, G * OFF * PH * CG)

    part = np.arange(128)
    copy = part % 32 // K
    consts = np.zeros((128, 134), np.float32)
    consts[:, 0:128] = np.eye(128)
    consts[:, 128] = np.where(copy >= 2, -1, 0)
    consts[:, 129] = -(copy % 2)
    consts[:, 130:134] = part[:, None] // 32 == np.arange(Q)

    def mixing(a):
        a = a[..., 0].transpose(0, 2, 1).reshape(K, Q, 1, C * C // Q).transpose(1, 2, 0, 3)
        return np.broadcast_to(a, (Q, 32 // K, K, C * C // Q)).reshape(128, C * C // Q)

    small = [
        cond.T,
        np.stack([w[p + n] for p in dense for n in ("W0", "W1")], axis=1),
        np.stack([by_phases(w[p + "c_weight"].T) for p in conv], axis=1),
        np.stack([w[p + n] for p in dense for n in ("b0", "b1")], axis=1),
        np.stack([w[p + "W2"] for p in dense], axis=1),
        np.broadcast_to(np.stack([w[p + "b2"] for p in dense]), (128, 2, K)),
        by_phases(side).T,
    ]
    arrays = {
        "x": x,
        "small": np.concatenate([a.reshape(128, -1) for a in small], axis=1),
        "mix_w": np.stack([mixing(w[p + "weight"]) for p in dense]),
        "mix_b": np.stack([w[p + "bias_k"] for p in dense], axis=1),
        "conv_w": np.stack([toeplitz(w[p + "weight"]) for p in conv]),
        "consts": consts,
    }
    arrays = {name: np.ascontiguousarray(a) for name, a in arrays.items()}
    nc = bacc.Bacc("TRN2", target_bir_lowering=False, num_devices=1)
    aps = {name: nc.dram_tensor(name, a.shape, mybir.dt.from_np(a.dtype), kind="ExternalInput").ap()
           for name, a in arrays.items()}
    scratch = nc.dram_tensor("mixed", (2, B, C * C), mybir.dt.float32, kind="Internal").ap()
    out = nc.dram_tensor("out", (B, C, T), mybir.dt.float32, kind="ExternalOutput").ap()
    build_cond_resid(nc, scratch=scratch, out=out, **aps)
    r = run_bass_kernel_spmd(nc, [arrays], core_ids=[0])
    return r.results[0]["out"]
```
